# Optimizing a Trainium2 kernel written in Bass

```python
import numpy as np
import jax
import jax.numpy as jnp

def _softmax(x, axis=-1):
    return jax.nn.softmax(x, axis=axis)

def _gelu(x):
    return jax.nn.gelu(x, approximate=True)

def _silu(x):
    return jax.nn.silu(x)

def _sigmoid(x):
    return jax.nn.sigmoid(x)

def _layernorm(x, axis=-1, eps=1e-05):
    m = jnp.mean(x, axis=axis, keepdims=True)
    v = jnp.var(x, axis=axis, keepdims=True)
    return (x - m) / jnp.sqrt(v + eps)

def _scatter_add(tgt, idx, src, axis=0):
    return tgt.at[idx].add(src)

def _segment_sum(src, seg, n):
    return jax.ops.segment_sum(src, seg, n)
kernel_name = 'mk_early_fusion_d1_tok_img2048_r4_4306a1'

def setup_inputs(seed: int=0):
    np.random.seed(seed)
    _w = jnp.asarray

    def _rec_inputs():
        import jax
        import jax.numpy as jnp
        _rk = jax.random.key(seed)
        x = -0.00178296 + 0.498989 * jax.random.normal(jax.random.fold_in(_rk, 1), (16, 256, 64, 2), jnp.float32)
        txt = 1.28965e-05 + 0.02 * jax.random.normal(jax.random.fold_in(_rk, 2), (16, 512, 512), jnp.float32)
        return (x, txt)
    x, txt = _rec_inputs()

    def _L0_tok_setup():
        import jax, jax.numpy as jnp
        import numpy as np
        H, N, CCH, LLEN = (256, 64, 1, 512)
        key = jax.random.key(seed)
        k1, k2 = jax.random.split(key, 2)
        log_dt = jax.random.uniform(k1, (H,), jnp.float32, float(np.log(0.001)), float(np.log(0.1)))
        C = 0.5 * jax.random.normal(k2, (CCH, H, N, 2), jnp.float32)
        log_w_real = jnp.full((H, N), float(np.log(0.5)), jnp.float32)
        w_imag = jnp.broadcast_to(np.pi * jnp.arange(N, dtype=jnp.float32), (H, N)) + jnp.zeros((H, N), jnp.float32)
        return {'C': C, 'log_dt': log_dt, 'log_w_real': log_w_real, 'w_imag': w_imag, 'L': LLEN}
    _L0_tok_all = _L0_tok_setup()
    _L0_tok_in = {k: v for k, v in _L0_tok_all.items() if k in ('log_dt', 'log_w_real', 'w_imag')}
    del _L0_tok_all

    def _L0_attn_setup():
        import jax, jax.numpy as jnp
        import numpy as np
        B, N, D = (4, 1024, 512)
        H = 16
        KH = 16
        DK = D // H
        key = jax.random.key(seed)
        kx, kq, kk, kv, ko = jax.random.split(key, 5)
        s = 1.0 / np.sqrt(D).astype(np.float32)
        return {'x': jax.random.normal(kx, (B, N, D), jnp.float32), 'Wq': jax.random.normal(kq, (D, D), jnp.float32) * s, 'Wk': jax.random.normal(kk, (D, D), jnp.float32) * s, 'Wv': jax.random.normal(kv, (D, D), jnp.float32) * s, 'Wo': jax.random.normal(ko, (D, D), jnp.float32) * s}
    _L0_attn_all = _L0_attn_setup()
    _L0_attn_in = {k: v for k, v in _L0_attn_all.items() if k in ('Wq', 'Wk', 'Wv', 'Wo')}
    del _L0_attn_all

    def _L0_ffn_setup():
        import jax, jax.numpy as jnp
        import numpy as np
        B_, S, D = (4, 1024, 512)
        OUT = 512
        E, R = (8, 16)
        ALPHA = 32.0
        SCALING = ALPHA / R
        key = jax.random.key(seed)
        ks = jax.random.split(key, 6)
        x = jax.random.normal(ks[0], (B_, S, D), dtype=jnp.float32)
        W_base = jax.random.normal(ks[1], (OUT, D), dtype=jnp.float32) * D ** (-0.5)
        b_base = jax.random.normal(ks[2], (OUT,), dtype=jnp.float32) * 0.01
        router_W = jax.random.normal(ks[3], (E, D), dtype=jnp.float32) * D ** (-0.5)
        A = jax.random.normal(ks[4], (E, R, D), dtype=jnp.float32) * D ** (-0.5)
        Bw = jax.random.normal(ks[5], (E, OUT, R), dtype=jnp.float32) * 0.02
        return {'x': x, 'W_base': W_base, 'b_base': b_base, 'router_W': router_W, 'A': A, 'Bw': Bw}
    _L0_ffn_all = _L0_ffn_setup()
    _L0_ffn_in = {k: v for k, v in _L0_ffn_all.items() if k in ('W_base', 'b_base', 'router_W', 'A', 'Bw')}
    del _L0_ffn_all
    return {'x': x, 'txt': txt, 'L0_tok_log_dt': _L0_tok_in['log_dt'], 'L0_tok_log_w_real': _L0_tok_in['log_w_real'], 'L0_tok_w_imag': _L0_tok_in['w_imag'], 'L0_attn_Wq': _L0_attn_in['Wq'], 'L0_attn_Wk': _L0_attn_in['Wk'], 'L0_attn_Wv': _L0_attn_in['Wv'], 'L0_attn_Wo': _L0_attn_in['Wo'], 'L0_ffn_W_base': _L0_ffn_in['W_base'], 'L0_ffn_b_base': _L0_ffn_in['b_base'], 'L0_ffn_router_W': _L0_ffn_in['router_W'], 'L0_ffn_A': _L0_ffn_in['A'], 'L0_ffn_Bw': _L0_ffn_in['Bw']}

def reference(x, txt, L0_tok_log_dt, L0_tok_log_w_real, L0_tok_w_imag, L0_attn_Wq, L0_attn_Wk, L0_attn_Wv, L0_attn_Wo, L0_ffn_W_base, L0_ffn_b_base, L0_ffn_router_W, L0_ffn_A, L0_ffn_Bw):
    import jax
    import jax.numpy as jnp

    def _L0_tok_ref(C, log_dt, log_w_real, w_imag, L):
        import jax, jax.numpy as jnp
        import numpy as np
        H, N, CCH, LLEN = (256, 64, 1, 512)
        dt = jnp.exp(log_dt)
        Cc = C[..., 0] + 1j * C[..., 1]
        w = -jnp.exp(log_w_real) + 1j * w_imag
        dtA = w * dt[:, None]
        K = dtA[:, :, None] * jnp.arange(L)
        Cm = Cc * (jnp.exp(dtA) - 1.0) / w
        K = jnp.einsum('chn,hnl->chl', Cm, jnp.exp(K))
        return 2 * K.real

    def _L0_attn_ref(x, Wq, Wk, Wv, Wo):
        import jax, jax.numpy as jnp
        import numpy as np
        B, N, D = (4, 1024, 512)
        H = 16
        KH = 16
        DK = D // H
        b, n, d = x.shape
        q = (x @ Wq).reshape(b, n, H, DK)
        k = (x @ Wk).reshape(b, n, KH, DK)
        v = (x @ Wv).reshape(b, n, KH, DK)
        scores = jnp.einsum('bnhd,bnkd->bnhk', q, k)
        o = jnp.einsum('bnhk,bnkd->bnhd', scores, v)
        return o.reshape(b, n, d) @ Wo

    def _L0_ffn_ref(x, W_base, b_base, router_W, A, Bw):
        import jax, jax.numpy as jnp
        import numpy as np
        B_, S, D = (4, 1024, 512)
        OUT = 512
        E, R = (8, 16)
        ALPHA = 32.0
        SCALING = ALPHA / R
        base_out = jnp.einsum('bsd,od->bso', x, W_base) + b_base
        logits = jnp.einsum('bsd,ed->bse', jax.lax.stop_gradient(x), router_W)
        routing_probs = jax.nn.softmax(logits, axis=-1)
        expert_idx = jnp.argmax(routing_probs, axis=-1)
        onehot = jax.nn.one_hot(expert_idx, E, dtype=x.dtype)
        h = jnp.einsum('bsd,erd->bser', x, A)
        h = h * onehot[..., None]
        delta = jnp.einsum('bser,eor->bso', h, Bw)
        return base_out + delta * SCALING
    h = _L0_tok_ref(x, L0_tok_log_dt, L0_tok_log_w_real, L0_tok_w_imag, 512)
    h = jnp.concatenate([h, txt], axis=1)
    h = h + _L0_attn_ref(_layernorm(h, axis=-1), L0_attn_Wq, L0_attn_Wk, L0_attn_Wv, L0_attn_Wo)
    h = h + _L0_ffn_ref(_layernorm(h, axis=-1), L0_ffn_W_base, L0_ffn_b_base, L0_ffn_router_W, L0_ffn_A, L0_ffn_Bw)
    return h

_drawn_inputs = setup_inputs


def setup_inputs(seed=0):
    import zlib

    import numpy as np

    out = dict(_drawn_inputs(seed))
    spreads = {'L0_tok_log_w_real': (-0.6931471824645996, 0.2)}
    factors = {'L0_ffn_b_base': 64.0, 'L0_ffn_router_W': 5.745, 'L0_ffn_A': 6.235, 'L0_ffn_Bw': 5.388}
    for name, (base, spread) in spreads.items():
        noise = np.random.default_rng([zlib.crc32(name.encode()), seed]).standard_normal(out[name].shape)
        drawn = base * np.exp(spread * noise) if base else spread * noise
        out[name] = jnp.asarray(drawn.astype(out[name].dtype))
    for name, factor in factors.items():
        out[name] = (out[name] * factor).astype(out[name].dtype)
    return out
```

```python
import concourse.bass as bass
from concourse import mybir
from contextlib import ExitStack
import numpy as np

P = 128
B, CH, NS, L = 16, 256, 64, 512
TXT = 512
D = L
NC_ = D // P
H, DK = 16, 32
EX, R = 8, 16
ROWS = CH + TXT
TXT_TILES = B * TXT // P
TOK_TILES = B * CH // P
TILES = TXT_TILES + TOK_TILES
HSLOTS = 4
J = P // DK
TG = P // H
G = DK // TG
LH = D // P
GC = 16
CHUNKS = CH // GC
EPS = 1e-5
SCALING = 32.0 / R
MAGIC = 12582912.0
LOG2E = float(np.float32(np.log2(np.e)))
LN2_HI = 0.693359375
LN2_LO = float(np.log(2.0) - LN2_HI)
TWO_PI = 2.0 * np.pi
PI2_HI = 6.28125
PI2_LO = float(TWO_PI - PI2_HI)
SIN_SCALE = 6.283185
QUARTER_TURN = 1.5707962


def fusion_kernel(nc, c_parts, txt, log_dt, log_w_real_t, w_imag_t, wq, wk, wv, wo, w_base_t, b_base,
                  router_t, a_t, bw_t, out):
    f32, f32r, i32 = mybir.dt.float32, mybir.dt.float32r, mybir.dt.int32
    ALU = mybir.AluOpType
    ACT = mybir.ActivationFunctionType
    AX = mybir.AxisListType.X

    txt_rows = txt.rearrange("b n d -> (b n) d")
    out_rows = out.rearrange("b n d -> (b n) d")
    tok = nc.dram_tensor("tok_rows", (B, CH, L), f32).ap()
    tok_rows = tok.rearrange("b h l -> (b h) l")

    ctx = ExitStack()
    with ctx:
        def sb(name, shape, dt=f32):
            return ctx.enter_context(nc.sbuf_tensor(name, shape, dt))

        def sem(name):
            return ctx.enter_context(nc.semaphore(name))

        ident = sb("ident", [P, P])
        diag = sb("diag", [P, J * P])
        prio = sb("prio", [P, EX])
        bias_rows = sb("bias_rows", [P, D])
        w_hi = {n: sb(f"w_hi_{n}", [P, NC_, D], f32r) for n in ("k", "v", "q", "o", "b")}
        w_lo = {n: sb(f"w_lo_{n}", [P, NC_, D], f32r) for n in ("k", "v", "q", "o", "b")}
        up_hi = sb("up_hi", [P, D], f32r)
        up_lo = sb("up_lo", [P, D], f32r)
        ar = sb("ar", [P, NC_, P + EX])

        h_in = sb("h_in", [P, HSLOTS, D])
        xn = sb("xn", [P, D])
        x_hi = sb("x_hi", [P, NC_, P], f32r)
        x_lo = sb("x_lo", [P, NC_, P], f32r)
        k_pad = sb("k_pad", [P, J, G * P])
        w_stage = k_pad[:, :, :].rearrange("p j n -> p (j n)")
        q_turn = sb("q_turn", [P, G * P])
        v_turn = sb("v_turn", [P, G * P])
        v_rows = sb("v_rows", [P, G, P])
        probs = sb("probs", [P, G, J * P])
        o_tok = sb("o_tok", [P, D])
        o_hi = sb("o_hi", [P, NC_, P], f32r)
        o_lo = sb("o_lo", [P, NC_, P], f32r)
        h1 = sb("h1", [P, 2, D])
        h1b = sb("h1b", [P, 2, D])
        xn2 = sb("xn2", [P, D])
        x2_f = sb("x2_f", [P, NC_, P])
        x2_hi = sb("x2_hi", [P, NC_, P], f32r)
        x2_lo = sb("x2_lo", [P, NC_, P], f32r)
        hm = sb("hm", [P, P])
        hm_hi = sb("hm_hi", [P, P], f32r)
        hm_lo = sb("hm_lo", [P, P], f32r)
        out_sb = sb("out_sb", [P, 2, D])
        stats = sb("stats", [P, 6])
        mv = sb("mv", [P, 2])
        ln = sb("ln", [P, 8])
        best = sb("best", [P, 2])
        ranked = sb("ranked", [P, EX])
        onehot = sb("onehot", [P, EX])

        pos = sb("pos", [P, P])
        quarter = sb("quarter", [P, 2])
        turns = sb("turns", [P, CH])
        decay = sb("decay", [P, CH])
        x1 = sb("x1", [P, CH, LH])
        x2 = sb("x2", [P, CH, LH])
        big = sb("big", [P, 3, GC * P])
        ul, ex, sn = big[:, 0, :], big[:, 1, :], big[:, 2, :]
        gbuf = sb("gbuf", [P, 2, GC, LH, B])
        cc = sb("cc", [P, 2, GC, B])
        g_out = sb("g_out", [P, 2, 4 * P])

        bank = [ctx.enter_context(nc.psum_tensor(f"bank{i}", [P, 512], f32)) for i in range(8)]
        k_bank, v_bank, q_bank, wo_bank, vt_bank = bank[:5]
        lora_bank, y_bank, ot_bank, x2t_bank, pv_bank = k_bank, v_bank, q_bank, wo_bank, vt_bank
        s_bank = [bank[5], bank[6], bank[7], bank[5]]
        xt_bank, gen_bank = bank[6], bank[7]

        h_loaded = [sem(f"h_loaded{i}") for i in range(HSLOTS)]
        stored = [sem(f"stored{i}") for i in range(2)]
        w_loaded, small_loaded, par_loaded = sem("w_loaded"), sem("small_loaded"), sem("par_loaded")
        w_hi_ready, w_lo_ready = sem("w_hi_ready"), sem("w_lo_ready")
        ident_made, consts_made, pads_zeroed = sem("ident_made"), sem("consts_made"), sem("pads_zeroed")
        dve_done = sem("dve_done")
        xn_ready, xt_done, x_hi_ready, x_lo_ready = sem("xn_ready"), sem("xt_done"), sem("x_hi_ready"), sem("x_lo_ready")
        k_done, v_done, q_done = sem("k_done"), sem("v_done"), sem("q_done")
        k_turned, v_turned, q_turned = sem("k_turned"), sem("v_turned"), sem("q_turned")
        vt_done, v_rows_ready, s_done, probs_ready = sem("vt_done"), sem("v_rows_ready"), sem("s_done"), sem("probs_ready")
        pv_done, o_tok_ready, ot_done, o_hi_ready, o_lo_ready = (sem("pv_done"), sem("o_tok_ready"), sem("ot_done"),
                                                                 sem("o_hi_ready"), sem("o_lo_ready"))
        wo_done, h1_ready, h1b_ready, xn2_ready = sem("wo_done"), sem("h1_ready"), sem("h1b_ready"), sem("xn2_ready")
        x2t_done, x2_f_ready, x2_hi_ready, x2_lo_ready = (sem("x2t_done"), sem("x2_f_ready"), sem("x2_hi_ready"),
                                                          sem("x2_lo_ready"))
        lora_done, hm_ready, hmt_done, hm_hi_ready, hm_lo_ready = (sem("lora_done"), sem("hm_ready"), sem("hmt_done"),
                                                                   sem("hm_hi_ready"), sem("hm_lo_ready"))
        y_done, out_ready = sem("y_done"), sem("out_ready")
        par_sin, par_exp = sem("par_sin"), sem("par_exp")
        par_args, par_ready = sem("par_args"), sem("par_ready")
        cc_loaded, g_args, g_decay_args = sem("cc_loaded"), sem("g_args"), sem("g_decay_args")
        g_wrapped, g_exp, g_sin, g_e2, g_g, g_prod = (sem("g_wrapped"), sem("g_exp"), sem("g_sin"), sem("g_e2"),
                                                      sem("g_g"), sem("g_prod"))
        g_mm, g_evac, tok_stored = sem("g_mm"), sem("g_evac"), sem("tok_stored")

        block = ctx.enter_context(nc.Block())

        def main_steps(e, step):
            for s in range(4):
                step(s, s)
            with e.Fori(1, TILES // 4 - 1) as it:
                for u in range(4):
                    step(it * 4 + u, u)
            for s in range(TILES - 4, TILES + 2):
                step(s, s % 4)

        def chunk_steps(e, chunk):
            chunk(0)
            with e.Fori(1, CHUNKS) as i:
                chunk(i)

        def known(s):
            return isinstance(s, int)

        def has(s, tile):
            return not known(s) or 0 <= tile < TILES

        def wait(e, s, value):
            if not known(value) or value > 0:
                e.wait_ge(s, value)

        @block.sync
        def _(sp):
            for half in range(2):
                rows = slice(half * NS, half * NS + NS)
                sp.dma_start(big[rows, 0, 0:CH], log_dt.rearrange("(a h) -> a h", a=1).to_broadcast((NS, CH))
                             ).then_inc(par_loaded, 16)
                sp.dma_start(big[rows, 0, CH:2 * CH], log_w_real_t).then_inc(par_loaded, 16)
                sp.dma_start(big[rows, 0, 2 * CH:3 * CH], w_imag_t).then_inc(par_loaded, 16)
            for n, w in enumerate((wk, wv, wq, wo, w_base_t)):
                if n:
                    sp.wait_ge(w_hi_ready, n)
                    sp.wait_ge(w_lo_ready, n)
                sp.dma_start(w_stage.rearrange("p (c n) -> p c n", c=NC_),
                             w.rearrange("(c p) n -> p c n", p=P)).then_inc(w_loaded, 16)
            sp.wait_ge(w_hi_ready, 5)
            sp.wait_ge(w_lo_ready, 5)
            sp.dma_start(w_stage[:, 0:D], bw_t).then_inc(w_loaded, 16)
            sp.dma_start(ar[:, :, 0:P], a_t.rearrange("(c p) n -> p c n", p=P)).then_inc(small_loaded, 16)
            sp.dma_start(ar[:, :, P:P + EX], router_t.rearrange("(c p) n -> p c n", p=P)).then_inc(small_loaded, 16)
            sp.dma_start(bias_rows[:, :], b_base.rearrange("(a n) -> a n", a=1).to_broadcast((P, D))
                         ).then_inc(small_loaded, 16)
            for t in range(HSLOTS):
                sp.dma_start(h_in[:, t, :], txt_rows[t * P:(t + 1) * P, :]).then_inc(h_loaded[t], 16)

            def chunk(i):
                wait(sp, g_g, i)
                for part in range(2):
                    for half in range(2):
                        sp.dma_start(cc[half * NS:half * NS + NS, part, :, :],
                                     c_parts[part, :, bass.ds(i * GC, GC), :]).then_inc(cc_loaded, 16)
                sp.wait_ge(g_evac, i * 2 + 2)
                for m in range(2):
                    for half in range(2):
                        for a in range(LH):
                            src = g_out[half * 64 + a * B:half * 64 + a * B + B, m, :].rearrange(
                                "b (c l) -> b c l", c=4)
                            dst = tok[:, bass.ds(i * GC + (8 * m + half), 7), a * P:(a + 1) * P][:, 0:7:2, :]
                            sp.dma_start(dst, src).then_inc(tok_stored, 16)

            chunk_steps(sp, chunk)

            def load_store(p, u, load_src, load_row, store_row):
                if load_src is not None:
                    sp.wait_ge(h1_ready, p + 1)
                    sp.dma_start(h_in[:, u, :], load_src[bass.ds(load_row, P), :]).then_inc(h_loaded[u], 16)
                sp.wait_ge(out_ready, p + 1)
                sp.dma_start(out_rows[bass.ds(store_row, P), :], out_sb[:, u % 2, :]).then_inc(stored[u % 2], 16)

            per = TXT // P
            with sp.Fori(0, B - 1) as b:
                for u in range(per):
                    load_store(b * per + u, u, txt_rows, b * (per * P) + (u + HSLOTS) * P, b * ROWS + (CH + u * P))
            sp.wait_ge(tok_stored, CHUNKS * 16 * 2 * 2 * LH)
            for u in range(per):
                load_store(TXT_TILES - per + u, u, tok_rows, u * P, (B - 1) * ROWS + CH + u * P)
            with sp.Fori(0, TOK_TILES // 4 - 1) as i:
                for u in range(4):
                    load_store(i * 4 + (TXT_TILES + u), u, tok_rows, i * (4 * P) + (u + 4) * P,
                               i * (2 * ROWS) + ((u // 2) * ROWS + (u % 2) * P))
            for u in range(4):
                load_store(TILES - 4 + u, u, None, 0, (B - 2 + u // 2) * ROWS + (u % 2) * P)
            for i in range(2):
                sp.wait_ge(stored[i], 16 * TILES // 2)

        @block.gpsimd
        def _(pool):
            pool.memset(ident[:, :], 0.0).then_inc(ident_made, 1)
            pool.wait_ge(ident_made, 1)
            pool.affine_select(out=ident[:, :], in_=ident[:, :], compare_op=ALU.not_equal, fill=1.0, base=0,
                               pattern=[[-1, P]], channel_multiplier=1).then_inc(ident_made, 1)
            pool.iota(diag[:, :], pattern=[[0, J * H], [-1, TG]], base=0, channel_multiplier=1,
                      allow_small_or_imprecise_dtypes=True).then_inc(consts_made, 1)
            pool.iota(pos[:, :], pattern=[[1, P]], base=0, channel_multiplier=0,
                      allow_small_or_imprecise_dtypes=True).then_inc(consts_made, 1)
            pool.iota(prio[:, :], pattern=[[-1, EX]], base=EX, channel_multiplier=0,
                      allow_small_or_imprecise_dtypes=True).then_inc(consts_made, 1)
            pool.memset(quarter[:, :], 0.0).then_inc(consts_made, 1)
            pool.wait_ge(consts_made, 4)
            pool.memset(quarter[0:NS, 0:1], 0.25).then_inc(consts_made, 1)
            pool.memset(quarter[0:NS, 1:2], QUARTER_TURN).then_inc(consts_made, 1)

            def channels(t, i, inner):
                return t[:, bass.ds(i * GC, GC)].unsqueeze(2).to_broadcast((P, GC, inner))

            pool.wait_ge(par_ready, 1)
            pool.wait_ge(w_lo_ready, 6)
            pool.memset(k_pad[:, :, :], 0.0).then_inc(pads_zeroed, 1)
            def chunk(i):
                row = pos[:, :].unsqueeze(1).to_broadcast((P, GC, P))
                wait(pool, g_e2, i)
                pool.tensor_tensor(out=ul.rearrange("p (c l) -> p c l", c=GC), in0=row,
                                   in1=channels(turns, i, P), op=ALU.mult).then_inc(g_args, 1)
                wait(pool, g_mm, i * 2)
                pool.tensor_tensor(out=ex.rearrange("p (c l) -> p c l", c=GC), in0=row,
                                   in1=channels(decay, i, P), op=ALU.mult).then_inc(g_decay_args, 1)
                pool.wait_ge(cc_loaded, i * 64 + 64)
                for part, xx in ((0, x1), (1, x2)):
                    pool.tensor_tensor(
                        out=gbuf[:, part, :, :, :],
                        in0=cc[:, part, :, :].unsqueeze(2).to_broadcast((P, GC, LH, B)),
                        in1=xx[:, bass.ds(i * GC, GC), :].unsqueeze(3).to_broadcast((P, GC, LH, B)),
                        op=ALU.mult).then_inc(g_prod, 1)
                pool.wait_ge(g_prod, i * 2 + 2)
                pool.tensor_tensor(out=gbuf[:, 0, :, :, :], in0=gbuf[:, 0, :, :, :], in1=gbuf[:, 1, :, :, :],
                                   op=ALU.add).then_inc(g_g, 1)
                pool.wait_ge(g_exp, i + 1)
                pool.wait_ge(g_sin, i + 1)
                pool.tensor_tensor(out=ex, in0=ex, in1=sn, op=ALU.mult).then_inc(g_e2, 1)

            chunk_steps(pool, chunk)

            pool.wait_ge(small_loaded, 48)

            def step(s, u):
                if not has(s, s - 1):
                    return
                b2 = (u + 1) % 2
                pool.wait_ge(h1_ready, s)
                wait(pool, out_ready, s - 2)
                pool.tensor_tensor(out=h1b[:, b2, :], in0=h1[:, b2, :], in1=bias_rows[:, :],
                                   op=ALU.add).then_inc(h1b_ready, 1)

            main_steps(pool, step)

        @block.scalar
        def _(act):
            for n, name in enumerate(("k", "v", "q", "o", "b")):
                act.wait_ge(w_loaded, 16 * (n + 1))
                act.activation(w_hi[name][:, :, :].rearrange("p c n -> p (c n)"), w_stage[:, :],
                               ACT.Copy).then_inc(w_hi_ready, 1)
            act.wait_ge(w_loaded, 16 * 6)
            act.activation(up_hi[:, :], w_stage[:, 0:D], ACT.Copy).then_inc(w_hi_ready, 1)

            act.wait_ge(par_args, 1)
            act.activation(big[:, 1, 0:CH], decay[:, :], ACT.Tanh, scale=0.5).then_inc(par_exp, 1)
            for a in range(LH):
                act.activation(big[:, 1, (1 + a) * CH:(2 + a) * CH], decay[:, :], ACT.Exp,
                               scale=float(a * P)).then_inc(par_exp, 1)
            act.wait_ge(par_args, 2)
            act.activation(sn, sn, ACT.Sin, scale=SIN_SCALE).then_inc(par_sin, 1)
            act.activation(gbuf[:, 0, :, :, :].rearrange("p c a b -> p (c a b)")[:, 0:3 * CH],
                           gbuf[:, 0, :, :, :].rearrange("p c a b -> p (c a b)")[:, 0:3 * CH],
                           ACT.Sin, scale=SIN_SCALE).then_inc(par_sin, 1)

            def chunk(i):
                act.wait_ge(g_decay_args, i + 1)
                act.activation(ex, ex, ACT.Exp).then_inc(g_exp, 1)
                act.wait_ge(g_wrapped, i + 1)
                act.activation(sn, sn, ACT.Sin, scale=-SIN_SCALE, bias=quarter[:, 1:2]).then_inc(g_sin, 1)
                wait(act, tok_stored, i * (16 * 4 * LH))
                for m in range(2):
                    act.wait_ge(g_mm, i * 2 + (m + 1))
                    act.activation(g_out[:, m, :], gen_bank[:, :], ACT.Copy).then_inc(g_evac, 1)

            chunk_steps(act, chunk)

            def turn_out(dst, src, done, value, ready):
                act.wait_ge(done, value)
                act.activation(dst, src, ACT.Copy).then_inc(ready, 1)

            def flat(t):
                return t[:, :, :].rearrange("p c n -> p (c n)")

            def step(s, u):
                if has(s, s):
                    wait(act, pv_done, s)
                    turn_out(flat(v_rows), vt_bank[:, :], vt_done, s + 1, v_rows_ready)
                if has(s, s - 1):
                    turn_out(flat(x2_f), x2t_bank[:, :], x2t_done, s, x2_f_ready)
                    act.activation(flat(x2_hi), x2t_bank[:, :], ACT.Copy).then_inc(x2_hi_ready, 1)
                    turn_out(hm_hi[:, :], x2t_bank[:, 0:P], hmt_done, s, hm_hi_ready)
                if has(s, s):
                    turn_out(flat(o_hi), ot_bank[:, :], ot_done, s + 1, o_hi_ready)
                if has(s, s + 1):
                    turn_out(flat(x_hi), xt_bank[:, :], xt_done, s + 2, x_hi_ready)

            act.wait_ge(xt_done, 1)
            act.activation(flat(x_hi), xt_bank[:, :], ACT.Copy).then_inc(x_hi_ready, 1)
            main_steps(act, step)

        @block.vector
        def _(dve):
            chain = [0, 0]

            def link(ins):
                chain[1] += 1
                ins.then_inc(dve_done, 1)
                dve.wait_ge(dve_done, chain[0] + chain[1])

            tt, ts, stt = dve.tensor_tensor, dve.tensor_scalar, dve.scalar_tensor_tensor

            def weight_split(n, lo, hi, width):
                dve.wait_ge(w_hi_ready, n + 1)
                tt(out=lo, in0=w_stage[:, 0:width], in1=hi.bitcast(f32), op=ALU.subtract).then_inc(w_lo_ready, 1)

            for n, name in enumerate(("k", "v", "q", "o", "b")):
                weight_split(n, w_lo[name][:, :, :].rearrange("p c n -> p (c n)"),
                             w_hi[name][:, :, :].rearrange("p c n -> p (c n)"), NC_ * D)
            weight_split(5, up_lo[:, :], up_hi[:, :], D)

            dve.wait_ge(consts_made, 6)
            di = probs[:, 0, :]
            link(ts(di, diag[:, :], 1.0 / TG, None, ALU.mult))
            link(ts(probs[:, 1, :], di, MAGIC, MAGIC, ALU.add, ALU.subtract))
            link(tt(out=diag[:, :], in0=di, in1=probs[:, 1, :], op=ALU.is_equal))

            dve.wait_ge(par_loaded, 96)
            scr = probs[:, :, :].rearrange("p g n -> p (g n)")
            k2, f2, q2, e2 = (scr[:, i * 2 * CH:(i + 1) * 2 * CH] for i in range(4))
            logs = big[:, 0, 0:2 * CH]
            link(ts(k2, logs, LOG2E, MAGIC, ALU.mult, ALU.add))
            link(ts(k2, k2, MAGIC, None, ALU.subtract))
            link(ts(k2, k2, -126.0, 127.0, ALU.max, ALU.min))
            link(stt(out=f2, in0=k2, scalar=-LN2_HI, in1=logs, op0=ALU.mult, op1=ALU.add))
            link(stt(out=f2, in0=k2, scalar=-LN2_LO, in1=f2, op0=ALU.mult, op1=ALU.add))
            link(ts(q2, f2, 1.0 / 5040, None, ALU.mult))
            for c in (1.0 / 720, 1.0 / 120, 1.0 / 24, 1.0 / 6, 0.5, 1.0):
                link(stt(out=q2, in0=q2, scalar=c, in1=f2, op0=ALU.add, op1=ALU.mult))
            link(ts(e2.bitcast(i32), k2, 127.0, 8388608.0, ALU.add, ALU.mult))
            link(stt(out=k2, in0=q2, scalar=1.0, in1=e2, op0=ALU.add, op1=ALU.mult))
            dt, a_re = k2[:, 0:CH], k2[:, CH:2 * CH]
            w_im = big[:, 0, 2 * CH:3 * CH]
            tmp = [scr[:, i * CH:(i + 1) * CH] for i in range(2, 8)]
            stt(out=decay[:, :], in0=a_re, scalar=-1.0, in1=dt, op0=ALU.mult, op1=ALU.mult).then_inc(par_args, 1)
            dve.wait_ge(par_args, 1)
            link(tt(out=tmp[0], in0=w_im, in1=dt, op=ALU.mult))
            link(ts(tmp[1], tmp[0], 1.0 / TWO_PI, MAGIC, ALU.mult, ALU.add))
            link(ts(tmp[1], tmp[1], MAGIC, None, ALU.subtract))
            link(stt(out=tmp[0], in0=tmp[1], scalar=-PI2_HI, in1=tmp[0], op0=ALU.mult, op1=ALU.add))
            link(stt(out=tmp[0], in0=tmp[1], scalar=-PI2_LO, in1=tmp[0], op0=ALU.mult, op1=ALU.add))
            link(ts(turns[:, :], tmp[0], 1.0 / TWO_PI, None, ALU.mult))
            angles = gbuf[:, 0, :, :, :].rearrange("p c a b -> p (c a b)")[:, 0:3 * CH]
            spare = gbuf[:, 1, :, :, :].rearrange("p c a b -> p (c a b)")[:, 0:3 * CH]
            for cs in range(2):
                for a in range(LH):
                    link(ts(sn[:, (cs * LH + a) * CH:(cs * LH + a + 1) * CH], turns[:, :], float(a * P),
                            0.25 * (1 - cs), ALU.mult, ALU.add))
            link(ts(angles[:, 0:CH], turns[:, :], 1.0, 0.25, ALU.mult, ALU.add))
            link(ts(angles[:, CH:2 * CH], turns[:, :], 1.0, None, ALU.mult))
            link(ts(angles[:, 2 * CH:3 * CH], turns[:, :], 0.5, None, ALU.mult))
            wrap = w_stage
            dve.wait_ge(w_lo_ready, 6)
            link(ts(spare, angles, MAGIC, MAGIC, ALU.add, ALU.subtract))
            link(ts(wrap, sn, MAGIC, MAGIC, ALU.add, ALU.subtract))
            link(tt(out=angles, in0=angles, in1=spare, op=ALU.subtract))
            tt(out=sn, in0=sn, in1=wrap, op=ALU.subtract).then_inc(par_args, 1)
            dve.wait_ge(par_args, 2)
            link(tt(out=tmp[0], in0=a_re, in1=a_re, op=ALU.mult))
            link(tt(out=tmp[1], in0=w_im, in1=w_im, op=ALU.mult))
            link(tt(out=tmp[0], in0=tmp[0], in1=tmp[1], op=ALU.add))
            link(dve.reciprocal(tmp[0], tmp[0]))
            dve.wait_ge(par_exp, 1)
            th = big[:, 1, 0:CH]
            link(ts(tmp[1], th, -1.0, 1.0, ALU.mult, ALU.add))
            link(dve.reciprocal(tmp[1], tmp[1]))
            link(stt(out=tmp[1], in0=th, scalar=2.0, in1=tmp[1], op0=ALU.mult, op1=ALU.mult))
            dve.wait_ge(par_sin, 2)
            cos1, sin1, sinh1 = (angles[:, i * CH:(i + 1) * CH] for i in range(3))
            link(stt(out=tmp[2], in0=sinh1, scalar=-2.0, in1=sinh1, op0=ALU.mult, op1=ALU.mult))
            link(tt(out=tmp[3], in0=tmp[1], in1=cos1, op=ALU.mult))
            link(tt(out=tmp[2], in0=tmp[2], in1=tmp[3], op=ALU.add))
            link(stt(out=tmp[3], in0=tmp[1], scalar=1.0, in1=sin1, op0=ALU.add, op1=ALU.mult))
            fr, fi = spare[:, 0:CH], spare[:, CH:2 * CH]
            link(tt(out=tmp[4], in0=tmp[3], in1=w_im, op=ALU.mult))
            link(tt(out=tmp[5], in0=tmp[2], in1=a_re, op=ALU.mult))
            link(tt(out=tmp[4], in0=tmp[4], in1=tmp[5], op=ALU.subtract))
            link(tt(out=fr, in0=tmp[4], in1=tmp[0], op=ALU.mult))
            link(tt(out=tmp[4], in0=tmp[3], in1=a_re, op=ALU.mult))
            link(tt(out=tmp[5], in0=tmp[2], in1=w_im, op=ALU.mult))
            link(tt(out=tmp[4], in0=tmp[4], in1=tmp[5], op=ALU.add))
            link(stt(out=fi, in0=tmp[4], scalar=-1.0, in1=tmp[0], op0=ALU.mult, op1=ALU.mult))
            dve.wait_ge(par_exp, 1 + LH)
            ea = big[:, 1, CH:(1 + LH) * CH]
            link(tt(out=sn[:, 0:LH * CH], in0=sn[:, 0:LH * CH], in1=ea, op=ALU.mult))
            link(tt(out=sn[:, LH * CH:2 * LH * CH], in0=sn[:, LH * CH:2 * LH * CH], in1=ea, op=ALU.mult))
            er = sn[:, 0:LH * CH].rearrange("p (a h) -> p h a", a=LH)
            ei = sn[:, LH * CH:2 * LH * CH].rearrange("p (a h) -> p h a", a=LH)

            def over_a(t):
                return t.unsqueeze(2).to_broadcast((P, CH, LH))

            m1 = wrap[:, 0:LH * CH].rearrange("p (h a) -> p h a", a=LH)
            m2 = wrap[:, LH * CH:2 * LH * CH].rearrange("p (h a) -> p h a", a=LH)
            link(tt(out=m1, in0=er, in1=over_a(fr), op=ALU.mult))
            link(tt(out=m2, in0=ei, in1=over_a(fi), op=ALU.mult))
            link(tt(out=x1[:, :, :], in0=m1, in1=m2, op=ALU.subtract))
            link(tt(out=m1, in0=er, in1=over_a(fi), op=ALU.mult))
            link(tt(out=m2, in0=ei, in1=over_a(fr), op=ALU.mult))
            link(tt(out=x2[:, :, :], in0=m1, in1=m2, op=ALU.add))
            top, low = slice(0, NS), slice(NS, P)
            link(ts(m1[low], x1[low, :, :], -2.0, None, ALU.mult))
            link(ts(x1[top, :, :], x1[top, :, :], 2.0, None, ALU.mult))
            link(ts(x2[:, :, :], x2[:, :, :], -2.0, None, ALU.mult))
            link(ts(x1[low, :, :], x2[low, :, :], 1.0, None, ALU.mult))
            ts(x2[low, :, :], m1[low], 1.0, None, ALU.mult).then_inc(par_ready, 1)

            base = chain[0] + chain[1]

            def chunk(i):
                chain[:] = [base + i, 0]
                dve.wait_ge(g_args, i + 1)
                wait(dve, g_e2, i)
                link(ts(sn, ul, quarter[:, 0:1], MAGIC, ALU.add, ALU.add))
                stt(out=sn, in0=sn, scalar=MAGIC, in1=ul, op0=ALU.subtract, op1=ALU.subtract).then_inc(g_wrapped, 1)

            chunk_steps(dve, chunk)
            chain[:] = [base + CHUNKS, 0]

            def layernorm(src, dst):
                link(dve.bn_stats(stats[:, :], src))
                dve.memset(ln[:, 4:5], 0.0)
                link(dve.bn_aggr(mv[:, :], stats[:, :]))
                var, half, y, z = ln[:, 0:1], ln[:, 1:2], ln[:, 2:3], ln[:, 3:4]
                link(ts(var, mv[:, 1:2], EPS, None, ALU.add))
                ts(half, var, -0.5, None, ALU.mult)
                link(ts(y.bitcast(i32), var.bitcast(i32), -0.5, 1597463007.0, ALU.mult, ALU.add))
                for _ in range(3):
                    link(stt(out=z, in0=y, scalar=half, in1=y, op0=ALU.mult, op1=ALU.mult))
                    link(stt(out=y, in0=z, scalar=1.5, in1=y, op0=ALU.add, op1=ALU.mult))
                return ts(dst, src, mv[:, 0:1], y, ALU.subtract, ALU.mult)

            def flat(t):
                return t[:, :, :].rearrange("p c n -> p (c n)")

            def rest(lo, bank_, hi, hi_ready, value, lo_ready):
                dve.wait_ge(hi_ready, value)
                tt(out=lo, in0=bank_, in1=hi.bitcast(f32), op=ALU.subtract).then_inc(lo_ready, 1)

            def turned(t, rows=slice(0, P)):
                return t[rows].rearrange("p (g h t) -> p h g t", g=G, t=TG)

            def heads(t, rows=slice(0, P)):
                return t[rows].rearrange("p (h g t) -> p h g t", h=H, g=G)

            def step(s, u):
                if has(s, s - 2):
                    dve.wait_ge(y_done, s - 1)
                    dve.wait_ge(h1b_ready, s - 1)
                    wait(dve, stored[u % 2], ((s // 2 - 1) * 16) if known(s) else s * 8 - (8 * (u % 2) + 16))
                    tt(out=out_sb[:, u % 2, :], in0=y_bank[:, :], in1=h1b[:, u % 2, :],
                       op=ALU.add).then_inc(out_ready, 1)
                if has(s, s + 1):
                    v = (u + 1) % 4
                    dve.wait_ge(h_loaded[v], ((s + 1) // 4 + 1) * 16 if known(s) else (s + 1 - v) * 4 + 16)
                    dve.wait_ge(xt_done, s + 1)
                    layernorm(h_in[:, v, :], xn[:, :]).then_inc(xn_ready, 1)
                if has(s, s):
                    dve.wait_ge(k_done, s + 1)
                    wait(dve, s_done, s * G)
                    for j in range(J):
                        rows = slice(DK * j, DK * j + DK)
                        last = dve.transpose(turned(k_pad[:, j, :], rows), heads(k_bank[:, :], rows))
                    last.then_inc(k_turned, 1)
                    dve.wait_ge(v_done, s + 1)
                    wait(dve, vt_done, s)
                    dve.transpose(turned(v_turn[:, :]), heads(v_bank[:, :])).then_inc(v_turned, 1)
                    dve.wait_ge(q_done, s + 1)
                    dve.transpose(turned(q_turn[:, :]), heads(q_bank[:, :])).then_inc(q_turned, 1)
                if has(s, s - 1):
                    b2, v = (u + 1) % 2, (u - 1) % 4
                    dve.wait_ge(wo_done, s)
                    tt(out=h1[:, b2, :], in0=wo_bank[:, :], in1=h_in[:, v, :], op=ALU.add).then_inc(h1_ready, 1)
                    dve.wait_ge(h1_ready, s)
                    wait(dve, x2t_done, s - 1)
                    layernorm(h1[:, b2, :], xn2[:, :]).then_inc(xn2_ready, 1)
                if has(s, s):
                    wait(dve, pv_done, s)
                    for g in range(G):
                        dve.wait_ge(s_done, s * G + (g + 1))
                        tt(out=probs[:, g, :], in0=s_bank[g][:, :], in1=diag[:, :], op=ALU.mult
                           ).then_inc(probs_ready, 1)
                if has(s, s - 1):
                    rest(flat(x2_lo), x2t_bank[:, :], flat(x2_hi), x2_hi_ready, s, x2_lo_ready)
                if has(s, s):
                    dve.wait_ge(pv_done, s + 1)
                    dve.transpose(o_tok[:, :], pv_bank[:, :]).then_inc(o_tok_ready, 1)
                if has(s, s - 1):
                    dve.wait_ge(lora_done, s)
                    logits = lora_bank[:, P:P + EX]
                    link(dve.reduce_max(best[:, 0:1], logits, AX))
                    link(stt(out=ranked[:, :], in0=logits, scalar=best[:, 0:1], in1=prio[:, :],
                             op0=ALU.is_ge, op1=ALU.mult))
                    link(dve.reduce_max(best[:, 1:2], ranked[:, :], AX))
                    link(ts(onehot[:, :], ranked[:, :], best[:, 1:2], SCALING, ALU.is_equal, ALU.mult))
                    wait(dve, hmt_done, s - 1)
                    tt(out=hm[:, :].rearrange("p (e r) -> p e r", e=EX),
                       in0=lora_bank[:, 0:P].rearrange("p (e r) -> p e r", e=EX),
                       in1=onehot[:, :].unsqueeze(2).to_broadcast((P, EX, R)), op=ALU.mult).then_inc(hm_ready, 1)
                    rest(hm_lo[:, :], x2t_bank[:, 0:P], hm_hi[:, :], hm_hi_ready, s, hm_lo_ready)
                if has(s, s):
                    rest(flat(o_lo), ot_bank[:, :], flat(o_hi), o_hi_ready, s + 1, o_lo_ready)
                if has(s, s + 1):
                    rest(flat(x_lo), xt_bank[:, :], flat(x_hi), x_hi_ready, s + 2, x_lo_ready)

            dve.wait_ge(h_loaded[0], 16)
            layernorm(h_in[:, 0, :], xn[:, :]).then_inc(xn_ready, 1)
            rest(flat(x_lo), xt_bank[:, :], flat(x_hi), x_hi_ready, 1, x_lo_ready)

            LINKS = 24

            def counted(s, u):
                if not known(s):
                    chain[:] = [before_loop[0] + (s - 4) * LINKS, 0]
                step(s, u)
                if known(s):
                    before_loop[0] = chain[0] + chain[1]
                else:
                    assert chain[1] == LINKS

            before_loop = [0]
            for s in range(4):
                counted(s, s)
            with dve.Fori(1, TILES // 4 - 1) as it:
                for u in range(4):
                    counted(it * 4 + u, u)
            chain[:] = [before_loop[0] + (TILES - 8) * LINKS, 0]
            for s in range(TILES - 4, TILES + 2):
                counted(s, s % 4)

        @block.tensor
        def _(pe):
            def transposes(bank_, src):
                for c in range(NC_):
                    last = pe.transpose(bank_[:, c * P:(c + 1) * P], src[:, c * P:(c + 1) * P], ident[:, :])
                return last

            def project(bank_, hi, lo, name, stop=True):
                products = [(hi, w_hi[name]), (hi, w_lo[name]), (lo, w_hi[name])]
                for n, (x, w) in enumerate(products):
                    for c in range(NC_):
                        last = pe.matmul(bank_[:, :], x[:, c, :], w[:, c, :], start=(n == 0 and c == 0),
                                         stop=(stop and n == 2 and c == NC_ - 1))
                return last

            def chunk(i):
                pe.wait_ge(g_g, i + 1)
                pe.wait_ge(g_e2, i + 1)
                for m in range(2):
                    wait(pe, g_evac, i * 2 + m)
                    for c in range(8):
                        ch = 8 * m + c
                        rows = slice(64 * (c % 2), 64 * (c % 2) + 64)
                        last = pe.matmul(gen_bank[rows, (c // 2) * P:(c // 2 + 1) * P],
                                         gbuf[:, 0, ch, :, :].rearrange("p a b -> p (a b)"),
                                         ex[:, ch * P:(ch + 1) * P], start=True, stop=True)
                    last.then_inc(g_mm, 1)

            chunk_steps(pe, chunk)

            pe.wait_ge(ident_made, 2)
            pe.wait_ge(xn_ready, 1)
            transposes(xt_bank, xn).then_inc(xt_done, 1)
            pe.wait_ge(w_lo_ready, 6)
            pe.wait_ge(pads_zeroed, 1)
            pe.wait_ge(small_loaded, 48)

            def step(s, u):
                if has(s, s):
                    pe.wait_ge(x_hi_ready, s + 1)
                    pe.wait_ge(x_lo_ready, s + 1)
                    project(k_bank, x_hi, x_lo, "k").then_inc(k_done, 1)
                    wait(pe, out_ready, s - 1)
                    project(v_bank, x_hi, x_lo, "v").then_inc(v_done, 1)
                    wait(pe, o_lo_ready, s)
                    project(q_bank, x_hi, x_lo, "q").then_inc(q_done, 1)
                if has(s, s - 1):
                    pe.wait_ge(o_hi_ready, s)
                    pe.wait_ge(o_lo_ready, s)
                    project(wo_bank, o_hi, o_lo, "o").then_inc(wo_done, 1)
                if has(s, s):
                    pe.wait_ge(v_turned, s + 1)
                    transposes(vt_bank, v_turn).then_inc(vt_done, 1)
                    pe.wait_ge(k_turned, s + 1)
                    pe.wait_ge(q_turned, s + 1)
                    for g in range(G):
                        if g == 3:
                            pe.wait_ge(probs_ready, s * G + 1)
                        for j in range(J):
                            last = pe.matmul(s_bank[g][:, j * P:(j + 1) * P], k_pad[:, j, g * P:(g + 1) * P],
                                             q_turn[:, g * P:(g + 1) * P], start=True, stop=True)
                        last.then_inc(s_done, 1)
                if has(s, s - 1):
                    pe.wait_ge(xn2_ready, s)
                    transposes(x2t_bank, xn2).then_inc(x2t_done, 1)
                if has(s, s):
                    pe.wait_ge(v_rows_ready, s + 1)
                    for g in range(G):
                        pe.wait_ge(probs_ready, s * G + (g + 1))
                        for j in range(J):
                            dst = pv_bank[DK * j:DK * j + DK, :].rearrange("p (h g t) -> p h g t", h=H, g=G)
                            last = pe.matmul(dst[:, :, g, :], v_rows[:, g, DK * j:DK * j + DK],
                                             probs[:, g, j * P:(j + 1) * P], start=True, stop=True)
                    last.then_inc(pv_done, 1)
                if has(s, s - 1):
                    pe.wait_ge(x2_f_ready, s)
                    for c in range(NC_):
                        last = pe.matmul(lora_bank[:, 0:P + EX], x2_f[:, c, :], ar[:, c, :], start=(c == 0),
                                         stop=(c == NC_ - 1))
                    last.then_inc(lora_done, 1)
                    pe.wait_ge(x2_hi_ready, s)
                    pe.wait_ge(x2_lo_ready, s)
                    project(y_bank, x2_hi, x2_lo, "b", stop=False)
                    pe.wait_ge(hm_ready, s)
                    pe.transpose(x2t_bank[:, 0:P], hm[:, :], ident[:, :]).then_inc(hmt_done, 1)
                if has(s, s):
                    pe.wait_ge(o_tok_ready, s + 1)
                    transposes(ot_bank, o_tok).then_inc(ot_done, 1)
                if has(s, s + 1):
                    pe.wait_ge(xn_ready, s + 2)
                    transposes(xt_bank, xn).then_inc(xt_done, 1)
                if has(s, s - 1):
                    pe.wait_ge(hm_hi_ready, s)
                    pe.wait_ge(hm_lo_ready, s)
                    pe.matmul(y_bank[:, :], hm_hi[:, :], up_hi[:, :], start=False, stop=False)
                    pe.matmul(y_bank[:, :], hm_hi[:, :], up_lo[:, :], start=False, stop=False)
                    pe.matmul(y_bank[:, :], hm_lo[:, :], up_hi[:, :], start=False, stop=True).then_inc(y_done, 1)

            main_steps(pe, step)


def kernel(x, txt, L0_tok_log_dt, L0_tok_log_w_real, L0_tok_w_imag, L0_attn_Wq, L0_attn_Wk, L0_attn_Wv,
           L0_attn_Wo, L0_ffn_W_base, L0_ffn_b_base, L0_ffn_router_W, L0_ffn_A, L0_ffn_Bw):
    import concourse.bacc as bacc
    from concourse.bass_utils import run_bass_kernel_spmd

    def laid(a):
        return np.ascontiguousarray(a)

    arrays = {
        "c_parts": laid(np.transpose(np.asarray(x), (3, 2, 1, 0))),
        "txt": laid(txt),
        "log_dt": laid(L0_tok_log_dt),
        "log_w_real_t": laid(np.transpose(np.asarray(L0_tok_log_w_real))),
        "w_imag_t": laid(np.transpose(np.asarray(L0_tok_w_imag))),
        "wq": laid(L0_attn_Wq), "wk": laid(L0_attn_Wk), "wv": laid(L0_attn_Wv), "wo": laid(L0_attn_Wo),
        "w_base_t": laid(np.transpose(np.asarray(L0_ffn_W_base))),
        "b_base": laid(L0_ffn_b_base),
        "router_t": laid(np.transpose(np.asarray(L0_ffn_router_W))),
        "a_t": laid(np.transpose(np.asarray(L0_ffn_A).reshape(EX * R, D))),
        "bw_t": laid(np.transpose(np.asarray(L0_ffn_Bw), (0, 2, 1)).reshape(EX * R, D)),
    }
    nc = bacc.Bacc("TRN2", target_bir_lowering=False, num_devices=1)
    args = [nc.dram_tensor(f"in_{n}", a.shape, mybir.dt.from_np(a.dtype), kind="ExternalInput").ap()
            for n, a in arrays.items()]
    out = nc.dram_tensor("out_rows", (B, ROWS, D), mybir.dt.float32, kind="ExternalOutput").ap()
    fusion_kernel(nc, *args, out)
    r = run_bass_kernel_spmd(nc, [{f"in_{n}": a for n, a in arrays.items()}], core_ids=[0])
    return r.results[0]["out_rows"]
```

```python
import concourse.bass as bass
from concourse import mybir
from contextlib import ExitStack, contextmanager
import numpy as np

P = 128
B, CH, NS, L = 16, 256, 64, 512
TXT = 512
D = L
NC_ = D // P
H, DK = 16, 32
EX, R = 8, 16
ROWS = CH + TXT
TXT_TILES = B * TXT // P
TOK_TILES = B * CH // P
TILES = TXT_TILES + TOK_TILES
HSLOTS = 4
J = P // DK
TG = P // H
G = DK // TG
LH = D // P
GC = 16
CHUNKS = CH // GC
EPS = 1e-5
SCALING = 32.0 / R
MAGIC = 12582912.0
LOG2E = float(np.float32(np.log2(np.e)))
LN2_HI = 0.693359375
LN2_LO = float(np.log(2.0) - LN2_HI)
TWO_PI = 2.0 * np.pi
PI2_HI = 6.28125
PI2_LO = float(TWO_PI - PI2_HI)
SIN_SCALE = 6.283185
QUARTER_TURN = 1.5707962


def fusion_kernel(nc, c_parts, txt, log_dt, log_w_real_t, w_imag_t, wq, wk, wv, wo, w_base_t, b_base,
                  router_t, a_t, bw_t, out):
    f32, f32r, i32 = mybir.dt.float32, mybir.dt.float32r, mybir.dt.int32
    ALU = mybir.AluOpType
    ACT = mybir.ActivationFunctionType
    AX = mybir.AxisListType.X

    txt_rows = txt.rearrange("b n d -> (b n) d")
    out_rows = out.rearrange("b n d -> (b n) d")
    tok = nc.dram_tensor("tok_rows", (B, CH, L), f32).ap()
    tok_rows = tok.rearrange("b h l -> (b h) l")

    ctx = ExitStack()
    with ctx:
        def sb(name, shape, dt=f32):
            return ctx.enter_context(nc.sbuf_tensor(name, shape, dt))

        def sem(name):
            return ctx.enter_context(nc.semaphore(name))

        ident = sb("ident", [P, P])
        diag = sb("diag", [P, J * P])
        prio = sb("prio", [P, EX])
        bias_rows = sb("bias_rows", [P, D])
        w_hi = {n: sb(f"w_hi_{n}", [P, NC_, D], f32r) for n in ("k", "v", "q", "o", "b")}
        w_lo = {n: sb(f"w_lo_{n}", [P, NC_, D], f32r) for n in ("k", "v", "q", "o", "b")}
        up_hi = sb("up_hi", [P, D], f32r)
        up_lo = sb("up_lo", [P, D], f32r)
        ar = sb("ar", [P, NC_, P + EX])

        h_in = sb("h_in", [P, HSLOTS, D])
        xn = sb("xn", [P, D])
        x_hi = sb("x_hi", [P, NC_, P], f32r)
        x_lo = sb("x_lo", [P, NC_, P], f32r)
        k_pad = sb("k_pad", [P, J, G * P])
        q_turn = sb("q_turn", [P, G * P])
        v_turn = sb("v_turn", [P, G * P])
        v_rows = sb("v_rows", [P, G, P])
        probs = sb("probs", [P, G, J * P])
        o_tok = sb("o_tok", [P, D])
        o_hi = sb("o_hi", [P, NC_, P], f32r)
        o_lo = sb("o_lo", [P, NC_, P], f32r)
        h1 = sb("h1", [P, 2, D])
        h1b = sb("h1b", [P, 2, D])
        w_stage = [k_pad[:, 0:2, :], k_pad[:, 2:4, :], h1[:, :, :], h1b[:, :, :]]
        halves = [(n, c) for n in ("k", "v", "q", "o", "b") for c in (0, NC_ // 2)]
        xn2 = sb("xn2", [P, D])
        x2_f = sb("x2_f", [P, NC_, P])
        x2_hi = sb("x2_hi", [P, NC_, P], f32r)
        x2_lo = sb("x2_lo", [P, NC_, P], f32r)
        hm = sb("hm", [P, P])
        hm_hi = sb("hm_hi", [P, P], f32r)
        hm_lo = sb("hm_lo", [P, P], f32r)
        out_sb = sb("out_sb", [P, 2, D])
        stats = sb("stats", [P, 6])
        mv = sb("mv", [P, 2])
        ln = sb("ln", [P, 8])
        best = sb("best", [P, 2])
        ranked = sb("ranked", [P, EX])
        onehot = sb("onehot", [P, EX])

        pos = sb("pos", [P, P])
        quarter = sb("quarter", [P, 2])
        turns = sb("turns", [P, CH])
        decay = sb("decay", [P, CH])
        x1 = sb("x1", [P, CH, LH])
        x2 = sb("x2", [P, CH, LH])
        big = sb("big", [P, 3, GC * P])
        ul, ex, sn = big[:, 0, :], big[:, 1, :], big[:, 2, :]
        gbuf = sb("gbuf", [P, 2, GC, LH, B])
        cc = sb("cc", [P, 2, GC, B])
        g_out = sb("g_out", [P, 2, 4 * P])

        bank = [ctx.enter_context(nc.psum_tensor(f"bank{i}", [P, 512], f32)) for i in range(8)]
        k_bank, v_bank, q_bank, wo_bank, vt_bank = bank[:5]
        lora_bank, y_bank, ot_bank, x2t_bank, pv_bank = k_bank, v_bank, q_bank, wo_bank, vt_bank
        s_bank = [bank[5], bank[6], bank[7], bank[5]]
        xt_bank = bank[6]
        gen_bank = [vt_bank, wo_bank]

        h_loaded = [sem(f"h_loaded{i}") for i in range(HSLOTS)]
        stored = [sem(f"stored{i}") for i in range(2)]
        w_loaded = [sem(f"w_loaded{i}") for i in range(len(w_stage))]
        small_loaded, par_loaded = sem("small_loaded"), sem("par_loaded")
        w_hi_ready = sem("w_hi_ready")
        qkv_lo_ready, ob_lo_ready = sem("qkv_lo_ready"), sem("ob_lo_ready")
        ident_made, consts_made, pads_zeroed = sem("ident_made"), sem("consts_made"), sem("pads_zeroed")
        dve_done = sem("dve_done")
        xn_ready, xt_done, x_hi_ready, x_lo_ready = sem("xn_ready"), sem("xt_done"), sem("x_hi_ready"), sem("x_lo_ready")
        k_done, v_done, q_done = sem("k_done"), sem("v_done"), sem("q_done")
        k_turned, v_turned, q_turned = sem("k_turned"), sem("v_turned"), sem("q_turned")
        vt_done, v_rows_ready, s_done, probs_ready = sem("vt_done"), sem("v_rows_ready"), sem("s_done"), sem("probs_ready")
        pv_done, o_tok_ready, ot_done, o_hi_ready, o_lo_ready = (sem("pv_done"), sem("o_tok_ready"), sem("ot_done"),
                                                                 sem("o_hi_ready"), sem("o_lo_ready"))
        wo_done, h1_ready, h1b_ready, xn2_ready = sem("wo_done"), sem("h1_ready"), sem("h1b_ready"), sem("xn2_ready")
        x2t_done, x2_f_ready, x2_hi_ready, x2_lo_ready = (sem("x2t_done"), sem("x2_f_ready"), sem("x2_hi_ready"),
                                                          sem("x2_lo_ready"))
        lora_done, hm_ready, hmt_done, hm_hi_ready, hm_lo_ready = (sem("lora_done"), sem("hm_ready"), sem("hmt_done"),
                                                                   sem("hm_hi_ready"), sem("hm_lo_ready"))
        y_done, out_ready = sem("y_done"), sem("out_ready")
        par_sin, par_exp = sem("par_sin"), sem("par_exp")
        par_args, par_ready = sem("par_args"), sem("par_ready")
        cc_loaded, g_args, g_decay_args = sem("cc_loaded"), sem("g_args"), sem("g_decay_args")
        g_wrapped, g_exp, g_sin, g_e2, g_g, g_prod = (sem("g_wrapped"), sem("g_exp"), sem("g_sin"), sem("g_e2"),
                                                      sem("g_g"), sem("g_prod"))
        g_mm, g_evac, tok_stored = sem("g_mm"), sem("g_evac"), sem("tok_stored")

        block = ctx.enter_context(nc.Block())

        def main_steps(step, chunk, loop):
            for u in range(4):
                step(u, u)
                chunk(0, u)
            with loop(1, CHUNKS) as it:
                for u in range(4):
                    step(it * 4 + u, u)
                    chunk(it, u)
            with loop(CHUNKS, TILES // 4 - 1) as it:
                for u in range(4):
                    step(it * 4 + u, u)
            for s in range(TILES - 4, TILES + 2):
                step(s, s % 4)

        def known(s):
            return isinstance(s, int)

        def has(s, tile):
            return not known(s) or 0 <= tile < TILES

        def wait(e, s, value):
            if not known(value) or value > 0:
                e.wait_ge(s, value)

        @block.sync
        def _(sp):
            for half in range(2):
                rows = slice(half * NS, half * NS + NS)
                sp.dma_start(big[rows, 0, 0:CH], log_dt.rearrange("(a h) -> a h", a=1).to_broadcast((NS, CH))
                             ).then_inc(par_loaded, 16)
                sp.dma_start(big[rows, 0, CH:2 * CH], log_w_real_t).then_inc(par_loaded, 16)
                sp.dma_start(big[rows, 0, 2 * CH:3 * CH], w_imag_t).then_inc(par_loaded, 16)
            sp.dma_start(h_in[:, 0, :], txt_rows[0:P, :]).then_inc(h_loaded[0], 16)
            w_dram = {"k": wk, "v": wv, "q": wq, "o": wo, "b": w_base_t}

            def stage_free(n):
                if n >= 4:
                    sp.wait_ge(w_hi_ready, n - 3)
                    if n - 4 < 6:
                        sp.wait_ge(qkv_lo_ready, n - 3)
                    else:
                        sp.wait_ge(ob_lo_ready, n - 9)

            for n, (name, c) in enumerate(halves):
                stage_free(n)
                sp.dma_start(w_stage[n % 4], w_dram[name].rearrange("(c p) n -> p c n", p=P)[:, c:c + 2, :]
                             ).then_inc(w_loaded[n % 4], 16)
            stage_free(10)
            sp.dma_start(w_stage[2][:, 0, :], bw_t).then_inc(w_loaded[2], 16)
            sp.dma_start(ar[:, :, 0:P], a_t.rearrange("(c p) n -> p c n", p=P)).then_inc(small_loaded, 16)
            sp.dma_start(ar[:, :, P:P + EX], router_t.rearrange("(c p) n -> p c n", p=P)).then_inc(small_loaded, 16)
            sp.dma_start(bias_rows[:, :], b_base.rearrange("(a n) -> a n", a=1).to_broadcast((P, D))
                         ).then_inc(small_loaded, 16)
            for t in range(1, HSLOTS):
                sp.dma_start(h_in[:, t, :], txt_rows[t * P:(t + 1) * P, :]).then_inc(h_loaded[t], 16)

            def load_coefficients(i):
                wait(sp, g_g, i)
                for part in range(2):
                    for half in range(2):
                        sp.dma_start(cc[half * NS:half * NS + NS, part, :, :],
                                     c_parts[part, :, bass.ds(i * GC, GC), :]).then_inc(cc_loaded, 16)

            def store_generated(i):
                sp.wait_ge(g_evac, i * 2 + 2)
                for m in range(2):
                    for half in range(2):
                        for a in range(LH):
                            src = g_out[half * 64 + a * B:half * 64 + a * B + B, m, :].rearrange(
                                "b (c l) -> b c l", c=4)
                            dst = tok[:, bass.ds(i * GC + (8 * m + half), 7), a * P:(a + 1) * P][:, 0:7:2, :]
                            sp.dma_start(dst, src).then_inc(tok_stored, 16)

            def load_store(p, u, load_src, load_row, store_row):
                if load_src is not None:
                    sp.wait_ge(h1_ready, p + 1)
                    sp.dma_start(h_in[:, u, :], load_src[bass.ds(load_row, P), :]).then_inc(h_loaded[u], 16)
                sp.wait_ge(out_ready, p + 1)
                sp.dma_start(out_rows[bass.ds(store_row, P), :], out_sb[:, u % 2, :]).then_inc(stored[u % 2], 16)

            per = TXT // P
            chunk_stores = 16 * 2 * 2 * LH

            def text_round(b):
                load_coefficients(b)
                for u in range(per):
                    if u == 1:
                        store_generated(b)
                    load_store(b * per + u, u, txt_rows, b * (per * P) + (u + HSLOTS) * P, b * ROWS + (CH + u * P))

            text_round(0)
            with sp.Fori(1, B - 1) as b:
                text_round(b)
            load_coefficients(CHUNKS - 1)
            for u in range(per):
                if u == 0:
                    sp.wait_ge(tok_stored, (CHUNKS - 1) * chunk_stores)
                if u == 1:
                    store_generated(CHUNKS - 1)
                    sp.wait_ge(tok_stored, CHUNKS * chunk_stores)
                load_store(TXT_TILES - per + u, u, tok_rows, u * P, (B - 1) * ROWS + CH + u * P)
            with sp.Fori(0, TOK_TILES // 4 - 1) as i:
                for u in range(4):
                    load_store(i * 4 + (TXT_TILES + u), u, tok_rows, i * (4 * P) + (u + 4) * P,
                               i * (2 * ROWS) + ((u // 2) * ROWS + (u % 2) * P))
            for u in range(4):
                load_store(TILES - 4 + u, u, None, 0, (B - 2 + u // 2) * ROWS + (u % 2) * P)
            for i in range(2):
                sp.wait_ge(stored[i], 16 * TILES // 2)

        @block.gpsimd
        def _(pool):
            pool.memset(ident[:, :], 0.0).then_inc(ident_made, 1)
            pool.wait_ge(ident_made, 1)
            pool.affine_select(out=ident[:, :], in_=ident[:, :], compare_op=ALU.not_equal, fill=1.0, base=0,
                               pattern=[[-1, P]], channel_multiplier=1).then_inc(ident_made, 1)
            pool.iota(diag[:, :], pattern=[[0, J * H], [-1, TG]], base=0, channel_multiplier=1,
                      allow_small_or_imprecise_dtypes=True).then_inc(consts_made, 1)
            pool.iota(pos[:, :], pattern=[[1, P]], base=0, channel_multiplier=0,
                      allow_small_or_imprecise_dtypes=True).then_inc(consts_made, 1)
            pool.iota(prio[:, :], pattern=[[-1, EX]], base=EX, channel_multiplier=0,
                      allow_small_or_imprecise_dtypes=True).then_inc(consts_made, 1)
            pool.memset(quarter[:, :], 0.0).then_inc(consts_made, 1)
            pool.wait_ge(consts_made, 4)
            pool.memset(quarter[0:NS, 0:1], 0.25).then_inc(consts_made, 1)
            pool.memset(quarter[0:NS, 1:2], QUARTER_TURN).then_inc(consts_made, 1)

            def channels(t, i, inner):
                return t[:, bass.ds(i * GC, GC)].unsqueeze(2).to_broadcast((P, GC, inner))

            for n, (name, c) in enumerate(halves):
                if n >= 6:
                    pool.wait_ge(w_hi_ready, n + 1)
                    pool.tensor_tensor(out=w_lo[name][:, c:c + 2, :], in0=w_stage[n % 4],
                                       in1=w_hi[name][:, c:c + 2, :].bitcast(f32), op=ALU.subtract
                                       ).then_inc(ob_lo_ready, 1)
            pool.wait_ge(w_hi_ready, 11)
            pool.tensor_tensor(out=up_lo[:, :], in0=w_stage[2][:, 0, :], in1=up_hi[:, :].bitcast(f32),
                               op=ALU.subtract).then_inc(ob_lo_ready, 1)

            def chunk(i, u):
                row = pos[:, :].unsqueeze(1).to_broadcast((P, GC, P))
                if u == 0:
                    if known(i):
                        pool.wait_ge(par_ready, 1)
                    wait(pool, g_e2, i)
                    pool.tensor_tensor(out=ul.rearrange("p (c l) -> p c l", c=GC), in0=row,
                                       in1=channels(turns, i, P), op=ALU.mult).then_inc(g_args, 1)
                    wait(pool, g_mm, i * 2)
                    pool.tensor_tensor(out=ex.rearrange("p (c l) -> p c l", c=GC), in0=row,
                                       in1=channels(decay, i, P), op=ALU.mult).then_inc(g_decay_args, 1)
                if u == 1:
                    pool.wait_ge(cc_loaded, i * 64 + 64)
                    for part, xx in ((0, x1), (1, x2)):
                        pool.tensor_tensor(
                            out=gbuf[:, part, :, :, :],
                            in0=cc[:, part, :, :].unsqueeze(2).to_broadcast((P, GC, LH, B)),
                            in1=xx[:, bass.ds(i * GC, GC), :].unsqueeze(3).to_broadcast((P, GC, LH, B)),
                            op=ALU.mult).then_inc(g_prod, 1)
                    pool.wait_ge(g_prod, i * 2 + 2)
                    pool.tensor_tensor(out=gbuf[:, 0, :, :, :], in0=gbuf[:, 0, :, :, :], in1=gbuf[:, 1, :, :, :],
                                       op=ALU.add).then_inc(g_g, 1)
                    pool.wait_ge(g_exp, i + 1)
                    pool.wait_ge(g_sin, i + 1)
                    pool.tensor_tensor(out=ex, in0=ex, in1=sn, op=ALU.mult).then_inc(g_e2, 1)

            pool.wait_ge(w_hi_ready, 10)
            pool.wait_ge(ob_lo_ready, 4)
            pool.wait_ge(qkv_lo_ready, 6)
            pool.memset(k_pad[:, :, :], 0.0).then_inc(pads_zeroed, 1)

            def step(s, u):
                if not has(s, s - 1):
                    return
                b2 = (u + 1) % 2
                pool.wait_ge(h1_ready, s)
                if known(s) and s == 1:
                    pool.wait_ge(ob_lo_ready, 5)
                wait(pool, out_ready, s - 2)
                pool.tensor_tensor(out=h1b[:, b2, :], in0=h1[:, b2, :], in1=bias_rows[:, :],
                                   op=ALU.add).then_inc(h1b_ready, 1)

            pool.wait_ge(small_loaded, 48)
            main_steps(step, chunk, pool.Fori)

        @block.scalar
        def _(act):
            for n, (name, c) in enumerate(halves):
                act.wait_ge(w_loaded[n % 4], 16 * (n // 4 + 1))
                act.activation(w_hi[name][:, c:c + 2, :], w_stage[n % 4], ACT.Copy).then_inc(w_hi_ready, 1)
            act.wait_ge(w_loaded[2], 48)
            act.activation(up_hi[:, :], w_stage[2][:, 0, :], ACT.Copy).then_inc(w_hi_ready, 1)

            act.wait_ge(par_args, 1)
            act.activation(big[:, 1, 0:CH], decay[:, :], ACT.Tanh, scale=0.5).then_inc(par_exp, 1)
            for a in range(LH):
                act.activation(big[:, 1, (1 + a) * CH:(2 + a) * CH], decay[:, :], ACT.Exp,
                               scale=float(a * P)).then_inc(par_exp, 1)
            act.wait_ge(par_args, 2)
            act.activation(sn, sn, ACT.Sin, scale=SIN_SCALE).then_inc(par_sin, 1)
            act.activation(gbuf[:, 0, :, :, :].rearrange("p c a b -> p (c a b)")[:, 0:3 * CH],
                           gbuf[:, 0, :, :, :].rearrange("p c a b -> p (c a b)")[:, 0:3 * CH],
                           ACT.Sin, scale=SIN_SCALE).then_inc(par_sin, 1)

            def chunk(i, u):
                if u == 1:
                    act.wait_ge(g_decay_args, i + 1)
                    act.activation(ex, ex, ACT.Exp).then_inc(g_exp, 1)
                    act.wait_ge(g_wrapped, i + 1)
                    act.activation(sn, sn, ACT.Sin, scale=-SIN_SCALE, bias=quarter[:, 1:2]).then_inc(g_sin, 1)
                if u == 2:
                    wait(act, tok_stored, i * (16 * 4 * LH))
                    for m in range(2):
                        act.wait_ge(g_mm, i * 2 + (m + 1))
                        act.activation(g_out[:, m, :], gen_bank[m][:, :], ACT.Copy).then_inc(g_evac, 1)

            def turn_out(dst, src, done, value, ready):
                act.wait_ge(done, value)
                act.activation(dst, src, ACT.Copy).then_inc(ready, 1)

            def flat(t):
                return t[:, :, :].rearrange("p c n -> p (c n)")

            def step(s, u):
                if has(s, s):
                    wait(act, pv_done, s)
                    turn_out(flat(v_rows), vt_bank[:, :], vt_done, s + 1, v_rows_ready)
                if has(s, s - 1):
                    turn_out(flat(x2_f), x2t_bank[:, :], x2t_done, s, x2_f_ready)
                    act.activation(flat(x2_hi), x2t_bank[:, :], ACT.Copy).then_inc(x2_hi_ready, 1)
                    turn_out(hm_hi[:, :], x2t_bank[:, 0:P], hmt_done, s, hm_hi_ready)
                if has(s, s):
                    turn_out(flat(o_hi), ot_bank[:, :], ot_done, s + 1, o_hi_ready)
                if has(s, s + 1):
                    turn_out(flat(x_hi), xt_bank[:, :], xt_done, s + 2, x_hi_ready)

            act.wait_ge(xt_done, 1)
            act.activation(flat(x_hi), xt_bank[:, :], ACT.Copy).then_inc(x_hi_ready, 1)
            main_steps(step, chunk, act.Fori)

        @block.vector
        def _(dve):
            chain = [0, 0]

            def link(ins):
                chain[1] += 1
                ins.then_inc(dve_done, 1)
                dve.wait_ge(dve_done, chain[0] + chain[1])

            tt, ts, stt = dve.tensor_tensor, dve.tensor_scalar, dve.scalar_tensor_tensor

            for n, (name, c) in enumerate(halves[0:6]):
                dve.wait_ge(w_hi_ready, n + 1)
                tt(out=w_lo[name][:, c:c + 2, :], in0=w_stage[n % 4], in1=w_hi[name][:, c:c + 2, :].bitcast(f32),
                   op=ALU.subtract).then_inc(qkv_lo_ready, 1)

            dve.wait_ge(consts_made, 6)
            di = probs[:, 0, :]
            link(ts(di, diag[:, :], 1.0 / TG, None, ALU.mult))
            link(ts(probs[:, 1, :], di, MAGIC, MAGIC, ALU.add, ALU.subtract))
            link(tt(out=diag[:, :], in0=di, in1=probs[:, 1, :], op=ALU.is_equal))

            dve.wait_ge(par_loaded, 96)
            scr = probs[:, :, :].rearrange("p g n -> p (g n)")
            k2, f2, q2, e2 = (scr[:, i * 2 * CH:(i + 1) * 2 * CH] for i in range(4))
            logs = big[:, 0, 0:2 * CH]
            link(ts(k2, logs, LOG2E, MAGIC, ALU.mult, ALU.add))
            link(ts(k2, k2, MAGIC, None, ALU.subtract))
            link(ts(k2, k2, -126.0, 127.0, ALU.max, ALU.min))
            link(stt(out=f2, in0=k2, scalar=-LN2_HI, in1=logs, op0=ALU.mult, op1=ALU.add))
            link(stt(out=f2, in0=k2, scalar=-LN2_LO, in1=f2, op0=ALU.mult, op1=ALU.add))
            link(ts(q2, f2, 1.0 / 5040, None, ALU.mult))
            for c in (1.0 / 720, 1.0 / 120, 1.0 / 24, 1.0 / 6, 0.5, 1.0):
                link(stt(out=q2, in0=q2, scalar=c, in1=f2, op0=ALU.add, op1=ALU.mult))
            link(ts(e2.bitcast(i32), k2, 127.0, 8388608.0, ALU.add, ALU.mult))
            link(stt(out=k2, in0=q2, scalar=1.0, in1=e2, op0=ALU.add, op1=ALU.mult))
            dt, a_re = k2[:, 0:CH], k2[:, CH:2 * CH]
            w_im = big[:, 0, 2 * CH:3 * CH]
            tmp = [scr[:, i * CH:(i + 1) * CH] for i in range(2, 8)]
            stt(out=decay[:, :], in0=a_re, scalar=-1.0, in1=dt, op0=ALU.mult, op1=ALU.mult).then_inc(par_args, 1)
            dve.wait_ge(par_args, 1)
            link(tt(out=tmp[0], in0=w_im, in1=dt, op=ALU.mult))
            link(ts(tmp[1], tmp[0], 1.0 / TWO_PI, MAGIC, ALU.mult, ALU.add))
            link(ts(tmp[1], tmp[1], MAGIC, None, ALU.subtract))
            link(stt(out=tmp[0], in0=tmp[1], scalar=-PI2_HI, in1=tmp[0], op0=ALU.mult, op1=ALU.add))
            link(stt(out=tmp[0], in0=tmp[1], scalar=-PI2_LO, in1=tmp[0], op0=ALU.mult, op1=ALU.add))
            link(ts(turns[:, :], tmp[0], 1.0 / TWO_PI, None, ALU.mult))
            angles = gbuf[:, 0, :, :, :].rearrange("p c a b -> p (c a b)")[:, 0:3 * CH]
            spare = gbuf[:, 1, :, :, :].rearrange("p c a b -> p (c a b)")[:, 0:3 * CH]
            for cs in range(2):
                for a in range(LH):
                    link(ts(sn[:, (cs * LH + a) * CH:(cs * LH + a + 1) * CH], turns[:, :], float(a * P),
                            0.25 * (1 - cs), ALU.mult, ALU.add))
            link(ts(angles[:, 0:CH], turns[:, :], 1.0, 0.25, ALU.mult, ALU.add))
            link(ts(angles[:, CH:2 * CH], turns[:, :], 1.0, None, ALU.mult))
            link(ts(angles[:, 2 * CH:3 * CH], turns[:, :], 0.5, None, ALU.mult))
            link(ts(spare, angles, MAGIC, MAGIC, ALU.add, ALU.subtract))
            wraps = [t[:, :, :].rearrange("p h a -> p (h a)") for t in (x1, x2)]
            for cs in range(2):
                link(ts(wraps[cs], sn[:, cs * LH * CH:(cs + 1) * LH * CH], MAGIC, MAGIC, ALU.add, ALU.subtract))
            link(tt(out=angles, in0=angles, in1=spare, op=ALU.subtract))
            link(tt(out=sn[:, 0:LH * CH], in0=sn[:, 0:LH * CH], in1=wraps[0], op=ALU.subtract))
            tt(out=sn[:, LH * CH:], in0=sn[:, LH * CH:], in1=wraps[1], op=ALU.subtract).then_inc(par_args, 1)
            dve.wait_ge(par_args, 2)
            link(tt(out=tmp[0], in0=a_re, in1=a_re, op=ALU.mult))
            link(tt(out=tmp[1], in0=w_im, in1=w_im, op=ALU.mult))
            link(tt(out=tmp[0], in0=tmp[0], in1=tmp[1], op=ALU.add))
            link(dve.reciprocal(tmp[0], tmp[0]))
            dve.wait_ge(par_exp, 1)
            th = big[:, 1, 0:CH]
            link(ts(tmp[1], th, -1.0, 1.0, ALU.mult, ALU.add))
            link(dve.reciprocal(tmp[1], tmp[1]))
            link(stt(out=tmp[1], in0=th, scalar=2.0, in1=tmp[1], op0=ALU.mult, op1=ALU.mult))
            dve.wait_ge(par_sin, 2)
            cos1, sin1, sinh1 = (angles[:, i * CH:(i + 1) * CH] for i in range(3))
            link(stt(out=tmp[2], in0=sinh1, scalar=-2.0, in1=sinh1, op0=ALU.mult, op1=ALU.mult))
            link(tt(out=tmp[3], in0=tmp[1], in1=cos1, op=ALU.mult))
            link(tt(out=tmp[2], in0=tmp[2], in1=tmp[3], op=ALU.add))
            link(stt(out=tmp[3], in0=tmp[1], scalar=1.0, in1=sin1, op0=ALU.add, op1=ALU.mult))
            fr, fi = spare[:, 0:CH], spare[:, CH:2 * CH]
            link(tt(out=tmp[4], in0=tmp[3], in1=w_im, op=ALU.mult))
            link(tt(out=tmp[5], in0=tmp[2], in1=a_re, op=ALU.mult))
            link(tt(out=tmp[4], in0=tmp[4], in1=tmp[5], op=ALU.subtract))
            link(tt(out=fr, in0=tmp[4], in1=tmp[0], op=ALU.mult))
            link(tt(out=tmp[4], in0=tmp[3], in1=a_re, op=ALU.mult))
            link(tt(out=tmp[5], in0=tmp[2], in1=w_im, op=ALU.mult))
            link(tt(out=tmp[4], in0=tmp[4], in1=tmp[5], op=ALU.add))
            link(stt(out=fi, in0=tmp[4], scalar=-1.0, in1=tmp[0], op0=ALU.mult, op1=ALU.mult))
            dve.wait_ge(par_exp, 1 + LH)
            ea = big[:, 1, CH:(1 + LH) * CH]
            link(tt(out=sn[:, 0:LH * CH], in0=sn[:, 0:LH * CH], in1=ea, op=ALU.mult))
            link(tt(out=sn[:, LH * CH:2 * LH * CH], in0=sn[:, LH * CH:2 * LH * CH], in1=ea, op=ALU.mult))
            er = sn[:, 0:LH * CH].rearrange("p (a h) -> p h a", a=LH)
            ei = sn[:, LH * CH:2 * LH * CH].rearrange("p (a h) -> p h a", a=LH)

            def over_a(t):
                return t.unsqueeze(2).to_broadcast((P, CH, LH))

            m1 = ul[:, 0:LH * CH].rearrange("p (h a) -> p h a", a=LH)
            m2 = ul[:, LH * CH:2 * LH * CH].rearrange("p (h a) -> p h a", a=LH)
            link(tt(out=m1, in0=er, in1=over_a(fr), op=ALU.mult))
            link(tt(out=m2, in0=ei, in1=over_a(fi), op=ALU.mult))
            link(tt(out=x1[:, :, :], in0=m1, in1=m2, op=ALU.subtract))
            link(tt(out=m1, in0=er, in1=over_a(fi), op=ALU.mult))
            link(tt(out=m2, in0=ei, in1=over_a(fr), op=ALU.mult))
            link(tt(out=x2[:, :, :], in0=m1, in1=m2, op=ALU.add))
            top, low = slice(0, NS), slice(NS, P)
            link(ts(m1[low], x1[low, :, :], -2.0, None, ALU.mult))
            link(ts(x1[top, :, :], x1[top, :, :], 2.0, None, ALU.mult))
            link(ts(x2[:, :, :], x2[:, :, :], -2.0, None, ALU.mult))
            link(ts(x1[low, :, :], x2[low, :, :], 1.0, None, ALU.mult))
            ts(x2[low, :, :], m1[low], 1.0, None, ALU.mult).then_inc(par_ready, 1)

            def chunk(i, u):
                if u == 1:
                    dve.wait_ge(g_args, i + 1)
                    wait(dve, g_e2, i)
                    link(ts(sn, ul, quarter[:, 0:1], MAGIC, ALU.add, ALU.add))
                    stt(out=sn, in0=sn, scalar=MAGIC, in1=ul, op0=ALU.subtract, op1=ALU.subtract
                        ).then_inc(g_wrapped, 1)

            def layernorm(src, dst):
                link(dve.bn_stats(stats[:, :], src))
                dve.memset(ln[:, 4:5], 0.0)
                link(dve.bn_aggr(mv[:, :], stats[:, :]))
                var, half, y, z = ln[:, 0:1], ln[:, 1:2], ln[:, 2:3], ln[:, 3:4]
                link(ts(var, mv[:, 1:2], EPS, None, ALU.add))
                ts(half, var, -0.5, None, ALU.mult)
                link(ts(y.bitcast(i32), var.bitcast(i32), -0.5, 1597463007.0, ALU.mult, ALU.add))
                for _ in range(3):
                    link(stt(out=z, in0=y, scalar=half, in1=y, op0=ALU.mult, op1=ALU.mult))
                    link(stt(out=y, in0=z, scalar=1.5, in1=y, op0=ALU.add, op1=ALU.mult))
                return ts(dst, src, mv[:, 0:1], y, ALU.subtract, ALU.mult)

            def flat(t):
                return t[:, :, :].rearrange("p c n -> p (c n)")

            def rest(lo, bank_, hi, hi_ready, value, lo_ready):
                dve.wait_ge(hi_ready, value)
                tt(out=lo, in0=bank_, in1=hi.bitcast(f32), op=ALU.subtract).then_inc(lo_ready, 1)

            def turned(t, rows=slice(0, P)):
                return t[rows].rearrange("p (g h t) -> p h g t", g=G, t=TG)

            def heads(t, rows=slice(0, P)):
                return t[rows].rearrange("p (h g t) -> p h g t", h=H, g=G)

            def step(s, u):
                if has(s, s - 2):
                    dve.wait_ge(y_done, s - 1)
                    dve.wait_ge(h1b_ready, s - 1)
                    wait(dve, stored[u % 2], ((s // 2 - 1) * 16) if known(s) else s * 8 - (8 * (u % 2) + 16))
                    tt(out=out_sb[:, u % 2, :], in0=y_bank[:, :], in1=h1b[:, u % 2, :],
                       op=ALU.add).then_inc(out_ready, 1)
                if has(s, s + 1):
                    v = (u + 1) % 4
                    dve.wait_ge(h_loaded[v], ((s + 1) // 4 + 1) * 16 if known(s) else (s + 1 - v) * 4 + 16)
                    dve.wait_ge(xt_done, s + 1)
                    layernorm(h_in[:, v, :], xn[:, :]).then_inc(xn_ready, 1)
                if has(s, s):
                    dve.wait_ge(k_done, s + 1)
                    if known(s) and s == 0:
                        dve.wait_ge(pads_zeroed, 1)
                    wait(dve, s_done, s * G)
                    for j in range(J):
                        rows = slice(DK * j, DK * j + DK)
                        last = dve.transpose(turned(k_pad[:, j, :], rows), heads(k_bank[:, :], rows))
                    last.then_inc(k_turned, 1)
                    dve.wait_ge(v_done, s + 1)
                    wait(dve, vt_done, s)
                    dve.transpose(turned(v_turn[:, :]), heads(v_bank[:, :])).then_inc(v_turned, 1)
                    dve.wait_ge(q_done, s + 1)
                    dve.transpose(turned(q_turn[:, :]), heads(q_bank[:, :])).then_inc(q_turned, 1)
                if has(s, s - 1):
                    b2, v = (u + 1) % 2, (u - 1) % 4
                    dve.wait_ge(wo_done, s)
                    if known(s) and s == 1:
                        dve.wait_ge(ob_lo_ready, 5)
                    tt(out=h1[:, b2, :], in0=wo_bank[:, :], in1=h_in[:, v, :], op=ALU.add).then_inc(h1_ready, 1)
                    dve.wait_ge(h1_ready, s)
                    wait(dve, x2t_done, s - 1)
                    layernorm(h1[:, b2, :], xn2[:, :]).then_inc(xn2_ready, 1)
                if has(s, s):
                    wait(dve, pv_done, s)
                    for g in range(G):
                        dve.wait_ge(s_done, s * G + (g + 1))
                        tt(out=probs[:, g, :], in0=s_bank[g][:, :], in1=diag[:, :], op=ALU.mult
                           ).then_inc(probs_ready, 1)
                if has(s, s - 1):
                    rest(flat(x2_lo), x2t_bank[:, :], flat(x2_hi), x2_hi_ready, s, x2_lo_ready)
                if has(s, s):
                    dve.wait_ge(pv_done, s + 1)
                    dve.transpose(o_tok[:, :], pv_bank[:, :]).then_inc(o_tok_ready, 1)
                if has(s, s - 1):
                    dve.wait_ge(lora_done, s)
                    logits = lora_bank[:, P:P + EX]
                    link(dve.reduce_max(best[:, 0:1], logits, AX))
                    link(stt(out=ranked[:, :], in0=logits, scalar=best[:, 0:1], in1=prio[:, :],
                             op0=ALU.is_ge, op1=ALU.mult))
                    link(dve.reduce_max(best[:, 1:2], ranked[:, :], AX))
                    link(ts(onehot[:, :], ranked[:, :], best[:, 1:2], SCALING, ALU.is_equal, ALU.mult))
                    wait(dve, hmt_done, s - 1)
                    tt(out=hm[:, :].rearrange("p (e r) -> p e r", e=EX),
                       in0=lora_bank[:, 0:P].rearrange("p (e r) -> p e r", e=EX),
                       in1=onehot[:, :].unsqueeze(2).to_broadcast((P, EX, R)), op=ALU.mult).then_inc(hm_ready, 1)
                    rest(hm_lo[:, :], x2t_bank[:, 0:P], hm_hi[:, :], hm_hi_ready, s, hm_lo_ready)
                if has(s, s):
                    rest(flat(o_lo), ot_bank[:, :], flat(o_hi), o_hi_ready, s + 1, o_lo_ready)
                if has(s, s + 1):
                    rest(flat(x_lo), xt_bank[:, :], flat(x_hi), x_hi_ready, s + 2, x_lo_ready)

            dve.wait_ge(h_loaded[0], 16)
            layernorm(h_in[:, 0, :], xn[:, :]).then_inc(xn_ready, 1)
            rest(flat(x_lo), xt_bank[:, :], flat(x_hi), x_hi_ready, 1, x_lo_ready)

            @contextmanager
            def linked_loop(first, last):
                before, links = chain[0] + chain[1], LINKS[first == 1]
                with dve.Fori(first, last) as it:
                    chain[:] = [before + (it - first) * links, 0]
                    yield it
                    assert chain[1] == links, chain[1]
                chain[:] = [before + (last - first) * links, 0]

            LINKS = {False: 4 * 24, True: 4 * 24 + 1}
            main_steps(step, chunk, linked_loop)

        @block.tensor
        def _(pe):
            def transposes(bank_, src):
                for c in range(NC_):
                    last = pe.transpose(bank_[:, c * P:(c + 1) * P], src[:, c * P:(c + 1) * P], ident[:, :])
                return last

            def project(bank_, hi, lo, name, stop=True):
                products = [(hi, w_hi[name]), (hi, w_lo[name]), (lo, w_hi[name])]
                for n, (x, w) in enumerate(products):
                    for c in range(NC_):
                        last = pe.matmul(bank_[:, :], x[:, c, :], w[:, c, :], start=(n == 0 and c == 0),
                                         stop=(stop and n == 2 and c == NC_ - 1))
                return last

            waits_evac = [None]

            def chunk(i, u):
                if u != 2:
                    return
                pe.wait_ge(g_g, i + 1)
                pe.wait_ge(g_e2, i + 1)
                for m in range(2):
                    for c in range(8):
                        ch = 8 * m + c
                        rows = slice(64 * (c % 2), 64 * (c % 2) + 64)
                        last = pe.matmul(gen_bank[m][rows, (c // 2) * P:(c // 2 + 1) * P],
                                         gbuf[:, 0, ch, :, :].rearrange("p a b -> p (a b)"),
                                         ex[:, ch * P:(ch + 1) * P], start=True, stop=True)
                    last.then_inc(g_mm, 1)
                waits_evac[0] = i

            pe.wait_ge(ident_made, 2)
            pe.wait_ge(xn_ready, 1)
            transposes(xt_bank, xn).then_inc(xt_done, 1)

            def step(s, u):
                if has(s, s):
                    pe.wait_ge(x_hi_ready, s + 1)
                    pe.wait_ge(x_lo_ready, s + 1)
                    if known(s) and s == 0:
                        pe.wait_ge(qkv_lo_ready, 2)
                    project(k_bank, x_hi, x_lo, "k").then_inc(k_done, 1)
                    if known(s) and s == 0:
                        pe.wait_ge(qkv_lo_ready, 4)
                    wait(pe, out_ready, s - 1)
                    project(v_bank, x_hi, x_lo, "v").then_inc(v_done, 1)
                    wait(pe, o_lo_ready, s)
                    if known(s) and s == 0:
                        pe.wait_ge(qkv_lo_ready, 6)
                    project(q_bank, x_hi, x_lo, "q").then_inc(q_done, 1)
                if waits_evac[0] is not None:
                    pe.wait_ge(g_evac, waits_evac[0] * 2 + 2)
                    waits_evac[0] = None
                if has(s, s - 1):
                    if known(s) and s == 1:
                        pe.wait_ge(ob_lo_ready, 5)
                        pe.wait_ge(small_loaded, 48)
                    pe.wait_ge(o_hi_ready, s)
                    pe.wait_ge(o_lo_ready, s)
                    project(wo_bank, o_hi, o_lo, "o").then_inc(wo_done, 1)
                if has(s, s):
                    pe.wait_ge(v_turned, s + 1)
                    transposes(vt_bank, v_turn).then_inc(vt_done, 1)
                    pe.wait_ge(k_turned, s + 1)
                    pe.wait_ge(q_turned, s + 1)
                    for g in range(G):
                        if g == 3:
                            pe.wait_ge(probs_ready, s * G + 1)
                        for j in range(J):
                            last = pe.matmul(s_bank[g][:, j * P:(j + 1) * P], k_pad[:, j, g * P:(g + 1) * P],
                                             q_turn[:, g * P:(g + 1) * P], start=True, stop=True)
                        last.then_inc(s_done, 1)
                if has(s, s - 1):
                    pe.wait_ge(xn2_ready, s)
                    transposes(x2t_bank, xn2).then_inc(x2t_done, 1)
                if has(s, s):
                    pe.wait_ge(v_rows_ready, s + 1)
                    for g in range(G):
                        pe.wait_ge(probs_ready, s * G + (g + 1))
                        for j in range(J):
                            dst = pv_bank[DK * j:DK * j + DK, :].rearrange("p (h g t) -> p h g t", h=H, g=G)
                            last = pe.matmul(dst[:, :, g, :], v_rows[:, g, DK * j:DK * j + DK],
                                             probs[:, g, j * P:(j + 1) * P], start=True, stop=True)
                    last.then_inc(pv_done, 1)
                if has(s, s - 1):
                    pe.wait_ge(x2_f_ready, s)
                    for c in range(NC_):
                        last = pe.matmul(lora_bank[:, 0:P + EX], x2_f[:, c, :], ar[:, c, :], start=(c == 0),
                                         stop=(c == NC_ - 1))
                    last.then_inc(lora_done, 1)
                    pe.wait_ge(x2_hi_ready, s)
                    pe.wait_ge(x2_lo_ready, s)
                    project(y_bank, x2_hi, x2_lo, "b", stop=False)
                    pe.wait_ge(hm_ready, s)
                    pe.transpose(x2t_bank[:, 0:P], hm[:, :], ident[:, :]).then_inc(hmt_done, 1)
                if has(s, s):
                    pe.wait_ge(o_tok_ready, s + 1)
                    transposes(ot_bank, o_tok).then_inc(ot_done, 1)
                if has(s, s + 1):
                    pe.wait_ge(xn_ready, s + 2)
                    transposes(xt_bank, xn).then_inc(xt_done, 1)
                if has(s, s - 1):
                    pe.wait_ge(hm_hi_ready, s)
                    pe.wait_ge(hm_lo_ready, s)
                    pe.matmul(y_bank[:, :], hm_hi[:, :], up_hi[:, :], start=False, stop=False)
                    pe.matmul(y_bank[:, :], hm_hi[:, :], up_lo[:, :], start=False, stop=False)
                    pe.matmul(y_bank[:, :], hm_lo[:, :], up_hi[:, :], start=False, stop=True).then_inc(y_done, 1)

            main_steps(step, chunk, pe.Fori)


def kernel(x, txt, L0_tok_log_dt, L0_tok_log_w_real, L0_tok_w_imag, L0_attn_Wq, L0_attn_Wk, L0_attn_Wv,
           L0_attn_Wo, L0_ffn_W_base, L0_ffn_b_base, L0_ffn_router_W, L0_ffn_A, L0_ffn_Bw):
    import concourse.bacc as bacc
    from concourse.bass_utils import run_bass_kernel_spmd

    def laid(a):
        return np.ascontiguousarray(a)

    arrays = {
        "c_parts": laid(np.transpose(np.asarray(x), (3, 2, 1, 0))),
        "txt": laid(txt),
        "log_dt": laid(L0_tok_log_dt),
        "log_w_real_t": laid(np.transpose(np.asarray(L0_tok_log_w_real))),
        "w_imag_t": laid(np.transpose(np.asarray(L0_tok_w_imag))),
        "wq": laid(L0_attn_Wq), "wk": laid(L0_attn_Wk), "wv": laid(L0_attn_Wv), "wo": laid(L0_attn_Wo),
        "w_base_t": laid(np.transpose(np.asarray(L0_ffn_W_base))),
        "b_base": laid(L0_ffn_b_base),
        "router_t": laid(np.transpose(np.asarray(L0_ffn_router_W))),
        "a_t": laid(np.transpose(np.asarray(L0_ffn_A).reshape(EX * R, D))),
        "bw_t": laid(np.transpose(np.asarray(L0_ffn_Bw), (0, 2, 1)).reshape(EX * R, D)),
    }
    nc = bacc.Bacc("TRN2", target_bir_lowering=False, num_devices=1)
    args = [nc.dram_tensor(f"in_{n}", a.shape, mybir.dt.from_np(a.dtype), kind="ExternalInput").ap()
            for n, a in arrays.items()]
    out = nc.dram_tensor("out_rows", (B, ROWS, D), mybir.dt.float32, kind="ExternalOutput").ap()
    fusion_kernel(nc, *args, out)
    r = run_bass_kernel_spmd(nc, [{f"in_{n}": a for n, a in arrays.items()}], core_ids=[0])
    return r.results[0]["out_rows"]
```

```python
import concourse.bass as bass
from concourse import mybir
from contextlib import ExitStack, contextmanager
import numpy as np

P = 128
B, CH, NS, L = 16, 256, 64, 512
TXT = 512
D = L
NC_ = D // P
H, DK = 16, 32
EX, R = 8, 16
ROWS = CH + TXT
TXT_TILES = B * TXT // P
TOK_TILES = B * CH // P
TILES = TXT_TILES + TOK_TILES
HSLOTS = 4
J = P // DK
TG = P // H
G = DK // TG
LH = D // P
GC = 16
CHUNKS = CH // GC
PREP = 2
EPS = 1e-5
SCALING = 32.0 / R
MAGIC = 12582912.0
LOG2E = float(np.float32(np.log2(np.e)))
LN2_HI = 0.693359375
LN2_LO = float(np.log(2.0) - LN2_HI)
TWO_PI = 2.0 * np.pi
PI2_HI = 6.28125
PI2_LO = float(TWO_PI - PI2_HI)
SIN_SCALE = 6.283185
QUARTER_TURN = 1.5707962


def fusion_kernel(nc, c_parts, txt, log_dt, log_w_real_t, w_imag_t, wq, wk, wv, wo, w_base_t, b_base,
                  router_t, a_t, bw_t, out):
    f32, f32r, i32 = mybir.dt.float32, mybir.dt.float32r, mybir.dt.int32
    ALU = mybir.AluOpType
    ACT = mybir.ActivationFunctionType
    AX = mybir.AxisListType.X

    txt_rows = txt.rearrange("b n d -> (b n) d")
    out_rows = out.rearrange("b n d -> (b n) d")
    tok = nc.dram_tensor("tok_rows", (B, CH, L), f32).ap()
    tok_rows = tok.rearrange("b h l -> (b h) l")

    ctx = ExitStack()
    with ctx:
        def sb(name, shape, dt=f32):
            return ctx.enter_context(nc.sbuf_tensor(name, shape, dt))

        def sem(name):
            return ctx.enter_context(nc.semaphore(name))

        ident = sb("ident", [P, P])
        diag = sb("diag", [P, J * P])
        prio = sb("prio", [P, EX])
        bias_rows = sb("bias_rows", [P, D])
        w_hi = {n: sb(f"w_hi_{n}", [P, NC_, D], f32r) for n in ("k", "v", "q", "o", "b")}
        w_lo = {n: sb(f"w_lo_{n}", [P, NC_, D], f32r) for n in ("k", "v", "q", "o", "b")}
        up_hi = sb("up_hi", [P, D], f32r)
        up_lo = sb("up_lo", [P, D], f32r)
        ar = sb("ar", [P, NC_, P + EX])

        h_in = sb("h_in", [P, HSLOTS, D])
        xn = sb("xn", [P, D])
        x_hi = sb("x_hi", [P, NC_, P], f32r)
        x_lo = sb("x_lo", [P, NC_, P], f32r)
        turn = sb("turn", [P, G * P])
        k_hi = sb("k_hi", [P, G * P], f32r)
        k_lo = sb("k_lo", [P, G * P], f32r)
        q_hi = sb("q_hi", [P, G, J * P], f32r)
        q_lo = sb("q_lo", [P, G, J * P], f32r)
        v_turn = sb("v_turn", [P, G * P])
        v_rows = sb("v_rows", [P, G, P])
        probs = sb("probs", [P, G, J * P])
        o_tok = sb("o_tok", [P, D])
        o_hi = sb("o_hi", [P, NC_, P], f32r)
        o_lo = sb("o_lo", [P, NC_, P], f32r)
        h1 = sb("h1", [P, 2, D])
        h1b = sb("h1b", [P, 2, D])
        halves = [(n, c) for n in ("k", "q", "v", "o", "b") for c in (0, NC_ // 2)]
        xn2 = sb("xn2", [P, D])
        x2_f = sb("x2_f", [P, NC_, P])
        x2_hi = sb("x2_hi", [P, NC_, P], f32r)
        x2_lo = sb("x2_lo", [P, NC_, P], f32r)
        hm = sb("hm", [P, P])
        hm_hi = sb("hm_hi", [P, P], f32r)
        hm_lo = sb("hm_lo", [P, P], f32r)
        out_sb = sb("out_sb", [P, 2, D])
        stats = sb("stats", [P, 6])
        mv = sb("mv", [P, 2])
        ln = sb("ln", [P, 8])
        best = sb("best", [P, 2])
        ranked = sb("ranked", [P, EX])
        onehot = sb("onehot", [P, EX])

        pos = sb("pos", [P, P])
        quarter = sb("quarter", [P, 2])
        turns = sb("turns", [P, CH])
        decay = sb("decay", [P, CH])
        x1 = sb("x1", [P, CH, LH])
        x2 = sb("x2", [P, CH, LH])
        big = sb("big", [P, 3, GC * P])
        ul, ex, sn = big[:, 0, :], big[:, 1, :], big[:, 2, :]
        gbuf = ul.rearrange("p (m c a b) -> p m c a b", m=2, c=GC, a=LH)
        io = sb("io", [P, 2 * GC * B + 2 * 4 * P])
        cc = io[:, 0:2 * GC * B].rearrange("p (m c b) -> p m c b", m=2, c=GC)
        g_out = io[:, 2 * GC * B:].rearrange("p (m n) -> p m n", m=2)
        w_stage = [t.rearrange("p (c n) -> p c n", c=NC_ // 2) for t in (
            ex[:, 0:2 * D], ex[:, 2 * D:4 * D], sn[:, 0:2 * D], sn[:, 2 * D:4 * D])] + [h1[:, :, :], h1b[:, :, :]]
        STAGES = len(w_stage)
        UP_STAGE = len(halves) % STAGES
        logs, w_im = big[:, 0, 0:2 * CH], big[:, 0, 2 * CH:3 * CH]
        tanh_half, decays_a = big[:, 1, 0:CH], big[:, 1, CH:(1 + LH) * CH]
        angles, spare = io[:, 0:3 * CH], io[:, 3 * CH:6 * CH]
        rest0, rest1 = big[:, 0, 3 * CH:8 * CH], big[:, 1, 5 * CH:8 * CH]
        k2, q2, f2, e2 = rest0[:, 0:2 * CH], rest0[:, 2 * CH:4 * CH], rest1[:, 0:2 * CH], x1[:, 0:CH // 2, :].rearrange(
            "p h a -> p (h a)")
        dt, a_re = k2[:, 0:CH], k2[:, CH:2 * CH]
        inverse, expm1 = logs[:, 0:CH], logs[:, CH:2 * CH]
        tmp = [q2[:, 0:CH], q2[:, CH:2 * CH], rest0[:, 4 * CH:5 * CH], f2[:, 0:CH], f2[:, CH:2 * CH],
               rest1[:, 2 * CH:3 * CH]]
        wraps = [t[:, :, :].rearrange("p h a -> p (h a)") for t in (x1, x2)]
        magic = sb("magic", [P, 1])

        bank = [ctx.enter_context(nc.psum_tensor(f"bank{i}", [P, 512], f32)) for i in range(8)]
        k_bank, y_bank, q_bank, wo_bank, vt_bank, xt_bank, v_bank = bank[0:5] + bank[6:8]
        lora_bank, ot_bank, x2t_bank, pv_bank = k_bank, q_bank, wo_bank, vt_bank
        s_bank = [bank[5], xt_bank, k_bank, q_bank]
        gen_bank = [vt_bank, v_bank]

        h_loaded = [sem(f"h_loaded{i}") for i in range(HSLOTS)]
        stored = [sem(f"stored{i}") for i in range(2)]
        w_loaded = [sem(f"w_loaded{i}") for i in range(len(w_stage))]
        small_loaded, par_loaded = sem("small_loaded"), sem("par_loaded")
        w_hi_ready = sem("w_hi_ready")
        qk_lo_ready, vob_lo_ready = sem("qk_lo_ready"), sem("vob_lo_ready")
        ident_made, consts_made, pads_zeroed = sem("ident_made"), sem("consts_made"), sem("pads_zeroed")
        dve_done = sem("dve_done")
        xn_ready, xt_done, x_hi_ready, x_lo_ready = sem("xn_ready"), sem("xt_done"), sem("x_hi_ready"), sem("x_lo_ready")
        k_done, v_done, q_done = sem("k_done"), sem("v_done"), sem("q_done")
        k_turned, v_turned, q_turned = sem("k_turned"), sem("v_turned"), sem("q_turned")
        k_hi_ready, k_lo_ready, q_hi_ready, q_lo_ready = (sem("k_hi_ready"), sem("k_lo_ready"), sem("q_hi_ready"),
                                                          sem("q_lo_ready"))
        vt_done, v_rows_ready, s_done, probs_ready = sem("vt_done"), sem("v_rows_ready"), sem("s_done"), sem("probs_ready")
        pv_done, o_tok_ready, ot_done, o_hi_ready, o_lo_ready = (sem("pv_done"), sem("o_tok_ready"), sem("ot_done"),
                                                                 sem("o_hi_ready"), sem("o_lo_ready"))
        wo_done, h1_ready, h1b_ready, xn2_ready = sem("wo_done"), sem("h1_ready"), sem("h1b_ready"), sem("xn2_ready")
        x2t_done, x2_f_ready, x2_hi_ready, x2_lo_ready = (sem("x2t_done"), sem("x2_f_ready"), sem("x2_hi_ready"),
                                                          sem("x2_lo_ready"))
        lora_done, hm_ready, hmt_done, hm_hi_ready, hm_lo_ready = (sem("lora_done"), sem("hm_ready"), sem("hmt_done"),
                                                                   sem("hm_hi_ready"), sem("hm_lo_ready"))
        y_done, out_ready = sem("y_done"), sem("out_ready")
        par_sin, par_exp = sem("par_sin"), sem("par_exp")
        par_scales, par_args, par_inverse = sem("par_scales"), sem("par_args"), sem("par_inverse")
        par_turns, par_rounded, par_wrapped = sem("par_turns"), sem("par_rounded"), sem("par_wrapped")
        par_expm1, par_made = sem("par_expm1"), sem("par_made")
        cc_loaded, g_args, g_decay_args = sem("cc_loaded"), sem("g_args"), sem("g_decay_args")
        g_wrapped, g_exp, g_sin, g_e2, g_g, g_prod = (sem("g_wrapped"), sem("g_exp"), sem("g_sin"), sem("g_e2"),
                                                      sem("g_g"), sem("g_prod"))
        g_mm, g_evac, tok_stored = sem("g_mm"), sem("g_evac"), sem("tok_stored")

        block = ctx.enter_context(nc.Block())

        def main_steps(step, prepare, chunk, loop):
            for s in range(4 * PREP):
                step(s, s % 4)
                prepare(s)
            for u in range(4):
                step(4 * PREP + u, u)
                chunk(0, u)
            with loop(PREP + 1, PREP + CHUNKS) as it:
                for u in range(4):
                    step(it * 4 + u, u)
                    chunk(it - PREP, u)
            with loop(PREP + CHUNKS, TILES // 4 - 1) as it:
                for u in range(4):
                    step(it * 4 + u, u)
            for s in range(TILES - 4, TILES + 2):
                step(s, s % 4)

        def known(s):
            return isinstance(s, int)

        def has(s, tile):
            return not known(s) or 0 <= tile < TILES

        def quarter_of(padded, j):
            return padded[DK * j:DK * j + DK, :, j * P:(j + 1) * P]

        def by_group(t, j):
            return t[DK * j:DK * j + DK, :].rearrange("p (g n) -> p g n", g=G)

        def wait(e, s, value):
            if not known(value) or value > 0:
                e.wait_ge(s, value)

        @block.sync
        def _(sp):
            sp.dma_start(h_in[:, 0, :], txt_rows[0:P, :]).then_inc(h_loaded[0], 16)
            w_dram = {"k": wk, "v": wv, "q": wq, "o": wo, "b": w_base_t}

            def stage_free(n):
                if n >= STAGES:
                    sp.wait_ge(w_hi_ready, n - STAGES + 1)
                    if n - STAGES < 4:
                        sp.wait_ge(qk_lo_ready, n - STAGES + 1)
                    else:
                        sp.wait_ge(vob_lo_ready, n - STAGES - 3)

            for n, (name, c) in enumerate(halves):
                if n == 4:
                    sp.dma_start(h_in[:, 1, :], txt_rows[P:2 * P, :]).then_inc(h_loaded[1], 16)
                if n == STAGES:
                    for half in range(2):
                        rows = slice(half * NS, half * NS + NS)
                        sp.dma_start(big[rows, 0, 0:CH], log_dt.rearrange("(a h) -> a h", a=1).to_broadcast((NS, CH))
                                     ).then_inc(par_loaded, 16)
                        sp.dma_start(big[rows, 0, CH:2 * CH], log_w_real_t).then_inc(par_loaded, 16)
                        sp.dma_start(big[rows, 0, 2 * CH:3 * CH], w_imag_t).then_inc(par_loaded, 16)
                stage_free(n)
                sp.dma_start(w_stage[n % STAGES], w_dram[name].rearrange("(c p) n -> p c n", p=P)[:, c:c + 2, :]
                             ).then_inc(w_loaded[n % STAGES], 16)
            stage_free(len(halves))
            sp.dma_start(w_stage[UP_STAGE][:, 0, :], bw_t).then_inc(w_loaded[UP_STAGE], 16)
            sp.dma_start(ar[:, :, 0:P], a_t.rearrange("(c p) n -> p c n", p=P)).then_inc(small_loaded, 16)
            sp.dma_start(ar[:, :, P:P + EX], router_t.rearrange("(c p) n -> p c n", p=P)).then_inc(small_loaded, 16)
            sp.dma_start(bias_rows[:, :], b_base.rearrange("(a n) -> a n", a=1).to_broadcast((P, D))
                         ).then_inc(small_loaded, 16)
            for t in range(2, HSLOTS):
                sp.dma_start(h_in[:, t, :], txt_rows[t * P:(t + 1) * P, :]).then_inc(h_loaded[t], 16)

            def load_coefficients(i):
                wait(sp, g_g, i)
                for part in range(2):
                    for half in range(2):
                        sp.dma_start(cc[half * NS:half * NS + NS, part, :, :],
                                     c_parts[part, :, bass.ds(i * GC, GC), :]).then_inc(cc_loaded, 16)

            def store_generated(i):
                sp.wait_ge(g_evac, i * 2 + 2)
                for m in range(2):
                    for half in range(2):
                        for a in range(LH):
                            src = g_out[half * 64 + a * B:half * 64 + a * B + B, m, :].rearrange(
                                "b (c l) -> b c l", c=4)
                            dst = tok[:, bass.ds(i * GC + (8 * m + half), 7), a * P:(a + 1) * P][:, 0:7:2, :]
                            sp.dma_start(dst, src).then_inc(tok_stored, 16)

            def load_store(p, u, load_src, load_row, store_row):
                if load_src is not None:
                    sp.wait_ge(h1_ready, p + 1)
                    sp.dma_start(h_in[:, u, :], load_src[bass.ds(load_row, P), :]).then_inc(h_loaded[u], 16)
                sp.wait_ge(out_ready, p + 1)
                sp.dma_start(out_rows[bass.ds(store_row, P), :], out_sb[:, u % 2, :]).then_inc(stored[u % 2], 16)

            chunk_stores = 16 * 2 * 2 * LH

            def text_rows_of(r, u):
                return r * (4 * P) + u * P, r * ROWS + (CH + u * P)

            def tok_rows_of(r, u, half):
                return r * (4 * CH) + (u * CH + half * P), r * (4 * ROWS) + (u * ROWS + half * P)

            def text_round(r, i=None):
                if i is not None:
                    load_coefficients(i)
                for u in range(4):
                    if i is not None and u == 1:
                        store_generated(i)
                    load_store(r * 4 + u, u, txt_rows, text_rows_of(r + 1, u)[0], text_rows_of(r, u)[1])

            text_rounds, half_rounds = TXT_TILES // 4, TOK_TILES // 8
            for r in range(PREP):
                text_round(r)
            text_round(PREP, 0)
            with sp.Fori(PREP + 1, text_rounds - 1) as r:
                text_round(r, r - PREP)
            r = text_rounds - 1
            load_coefficients(r - PREP)
            for u in range(4):
                if u == 0:
                    sp.wait_ge(tok_stored, (r - PREP) * chunk_stores)
                if u == 1:
                    store_generated(r - PREP)
                load_store(r * 4 + u, u, tok_rows, tok_rows_of(0, u, 0)[0], text_rows_of(r, u)[1])
            for r in range(PREP):
                load_coefficients(CHUNKS - PREP + r)
                for u in range(4):
                    if u == 1:
                        store_generated(CHUNKS - PREP + r)
                    load_store(TXT_TILES + r * 4 + u, u, tok_rows, tok_rows_of(r + 1, u, 0)[0],
                               tok_rows_of(r, u, 0)[1])
            for half in range(2):
                p0 = TXT_TILES + half * (TOK_TILES // 2)
                with sp.Fori(0 if half else PREP, half_rounds - 1) as r:
                    for u in range(4):
                        load_store(r * 4 + (p0 + u), u, tok_rows, tok_rows_of(r + 1, u, half)[0],
                                   tok_rows_of(r, u, half)[1])
                r = half_rounds - 1
                if half == 0:
                    sp.wait_ge(tok_stored, CHUNKS * chunk_stores)
                for u in range(4):
                    load_store(p0 + 4 * r + u, u, None if half else tok_rows, tok_rows_of(0, u, 1)[0],
                               tok_rows_of(r, u, half)[1])
            for i in range(2):
                sp.wait_ge(stored[i], 16 * TILES // 2)

        @block.gpsimd
        def _(pool):
            tt, ts = pool.tensor_tensor, pool.tensor_scalar
            pool.memset(ident[:, :], 0.0).then_inc(ident_made, 1)
            pool.wait_ge(ident_made, 1)
            pool.affine_select(out=ident[:, :], in_=ident[:, :], compare_op=ALU.not_equal, fill=1.0, base=0,
                               pattern=[[-1, P]], channel_multiplier=1).then_inc(ident_made, 1)
            pool.memset(q_hi[:, :, :].bitcast(f32), 0.0).then_inc(pads_zeroed, 1)
            pool.memset(q_lo[:, :, :].bitcast(f32), 0.0).then_inc(pads_zeroed, 1)
            pool.iota(diag[:, :], pattern=[[0, J * H], [-1, TG]], base=0, channel_multiplier=1,
                      allow_small_or_imprecise_dtypes=True).then_inc(consts_made, 1)
            pool.iota(pos[:, :], pattern=[[1, P]], base=0, channel_multiplier=0,
                      allow_small_or_imprecise_dtypes=True).then_inc(consts_made, 1)
            pool.iota(prio[:, :], pattern=[[-1, EX]], base=EX, channel_multiplier=0,
                      allow_small_or_imprecise_dtypes=True).then_inc(consts_made, 1)
            pool.memset(magic[:, :], MAGIC).then_inc(consts_made, 1)
            pool.memset(quarter[:, :], 0.0).then_inc(consts_made, 1)
            pool.wait_ge(consts_made, 5)
            pool.memset(quarter[0:NS, 0:1], 0.25).then_inc(consts_made, 1)
            pool.memset(quarter[0:NS, 1:2], QUARTER_TURN).then_inc(consts_made, 1)

            def channels(t, i, inner):
                return t[:, bass.ds(i * GC, GC)].unsqueeze(2).to_broadcast((P, GC, inner))

            for n, (name, c) in enumerate(halves):
                if n >= 4:
                    pool.wait_ge(w_hi_ready, n + 1)
                    pool.tensor_tensor(out=w_lo[name][:, c:c + 2, :], in0=w_stage[n % STAGES],
                                       in1=w_hi[name][:, c:c + 2, :].bitcast(f32), op=ALU.subtract
                                       ).then_inc(vob_lo_ready, 1)
            pool.wait_ge(w_hi_ready, 11)
            pool.tensor_tensor(out=up_lo[:, :], in0=w_stage[UP_STAGE][:, 0, :], in1=up_hi[:, :].bitcast(f32),
                               op=ALU.subtract).then_inc(vob_lo_ready, 1)

            def chunk(i, u):
                row = pos[:, :].unsqueeze(1).to_broadcast((P, GC, P))
                if u == 0:
                    wait(pool, g_e2, i)
                    wait(pool, g_mm, i * 2)
                    pool.tensor_tensor(out=ul.rearrange("p (c l) -> p c l", c=GC), in0=row,
                                       in1=channels(turns, i, P), op=ALU.mult).then_inc(g_args, 1)
                    pool.wait_ge(g_args, i * 3 + 1)
                    pool.tensor_tensor(out=ex.rearrange("p (c l) -> p c l", c=GC), in0=row,
                                       in1=channels(decay, i, P), op=ALU.mult).then_inc(g_decay_args, 1)
                    ts(sn, ul, quarter[:, 0:1], MAGIC, ALU.add, ALU.add).then_inc(g_args, 1)
                    pool.wait_ge(g_args, i * 3 + 2)
                    tt(out=sn, in0=sn, in1=magic[:, :].to_broadcast((P, GC * P)), op=ALU.subtract).then_inc(g_args, 1)
                    pool.wait_ge(g_args, i * 3 + 3)
                    tt(out=sn, in0=sn, in1=ul, op=ALU.subtract).then_inc(g_wrapped, 1)
                if u == 1:
                    pool.wait_ge(cc_loaded, i * 64 + 64)
                    pool.wait_ge(g_wrapped, i + 1)
                    for part, xx in ((0, x1), (1, x2)):
                        pool.tensor_tensor(
                            out=gbuf[:, part, :, :, :],
                            in0=cc[:, part, :, :].unsqueeze(2).to_broadcast((P, GC, LH, B)),
                            in1=xx[:, bass.ds(i * GC, GC), :].unsqueeze(3).to_broadcast((P, GC, LH, B)),
                            op=ALU.mult).then_inc(g_prod, 1)
                    pool.wait_ge(g_prod, i * 2 + 2)
                    pool.tensor_tensor(out=gbuf[:, 0, :, :, :], in0=gbuf[:, 0, :, :, :], in1=gbuf[:, 1, :, :, :],
                                       op=ALU.add).then_inc(g_g, 1)
                    pool.wait_ge(g_exp, i + 1)
                    pool.wait_ge(g_sin, i + 1)
                    pool.tensor_tensor(out=ex, in0=ex, in1=sn, op=ALU.mult).then_inc(g_e2, 1)

            def step(s, u):
                if not has(s, s - 1):
                    return
                b2 = (u + 1) % 2
                pool.wait_ge(h1_ready, s)
                if known(s) and s == 1:
                    pool.wait_ge(vob_lo_ready, 7)
                wait(pool, out_ready, s - 2)
                pool.tensor_tensor(out=h1b[:, b2, :], in0=h1[:, b2, :], in1=bias_rows[:, :],
                                   op=ALU.add).then_inc(h1b_ready, 1)

            pool.wait_ge(small_loaded, 48)

            made = [0]

            def link(ins):
                made[0] += 1
                ins.then_inc(par_made, 1)
                pool.wait_ge(par_made, made[0])

            def rounded(dst, src):
                link(ts(dst, src, MAGIC, None, ALU.add))
                link(ts(dst, dst, MAGIC, None, ALU.subtract))

            def horner(c):
                link(ts(q2, q2, c, None, ALU.add))
                link(tt(out=q2, in0=q2, in1=f2, op=ALU.mult))

            def exponentials_begun():
                pool.wait_ge(par_scales, 1)
                pool.wait_ge(vob_lo_ready, 7)
                for part, x in ((LN2_HI, logs), (LN2_LO, f2)):
                    link(ts(q2, k2, part, None, ALU.mult))
                    link(tt(out=f2, in0=x, in1=q2, op=ALU.subtract))
                link(ts(q2, f2, 1.0 / 5040, None, ALU.mult))
                horner(1.0 / 720)
                horner(1.0 / 120)

            def exponentials():
                for c in (1.0 / 24, 1.0 / 6, 0.5, 1.0):
                    horner(c)
                link(ts(q2, q2, 1.0, None, ALU.add))
                link(tt(out=k2, in0=q2, in1=e2, op=ALU.mult))
                tt(out=tmp[0], in0=a_re, in1=a_re, op=ALU.mult)
                tt(out=tmp[1], in0=w_im, in1=w_im, op=ALU.mult)
                link(tt(out=tmp[2], in0=a_re, in1=dt, op=ALU.mult))
                tt(out=tmp[0], in0=tmp[0], in1=tmp[1], op=ALU.add).then_inc(par_args, 1)
                ts(decay[:, :], tmp[2], -1.0, None, ALU.mult).then_inc(par_args, 1)

            def angle_args():
                pool.wait_ge(par_inverse, 1)
                pool.wait_ge(vob_lo_ready, 7)
                link(tt(out=tmp[0], in0=w_im, in1=dt, op=ALU.mult))
                link(ts(tmp[1], tmp[0], 1.0 / TWO_PI, None, ALU.mult))
                rounded(tmp[1], tmp[1])
                for part in (PI2_HI, PI2_LO):
                    link(ts(tmp[2], tmp[1], part, None, ALU.mult))
                    link(tt(out=tmp[0], in0=tmp[0], in1=tmp[2], op=ALU.subtract))
                link(ts(turns[:, :], tmp[0], 1.0 / TWO_PI, None, ALU.mult))
                for cs in range(2):
                    for a in range(LH):
                        ts(sn[:, (cs * LH + a) * CH:(cs * LH + a + 1) * CH], turns[:, :], float(a * P),
                           0.25 * (1 - cs), ALU.mult, ALU.add)
                ts(angles[:, 0:CH], turns[:, :], 1.0, 0.25, ALU.mult, ALU.add)
                ts(angles[:, CH:2 * CH], turns[:, :], 1.0, None, ALU.mult)
                ts(angles[:, 2 * CH:3 * CH], turns[:, :], 0.5, None, ALU.mult).then_inc(par_turns, 1)

            def wrapped():
                pool.wait_ge(par_rounded, 1)
                tt(out=angles, in0=angles, in1=spare, op=ALU.subtract)
                for cs in range(2):
                    part = sn[:, cs * LH * CH:(cs + 1) * LH * CH]
                    tt(out=part, in0=part, in1=wraps[cs], op=ALU.subtract).then_inc(par_wrapped, 1)

            fr, fi = spare[:, 0:CH], spare[:, CH:2 * CH]

            def one_step_factor():
                pool.wait_ge(par_wrapped, 2)
                pool.wait_ge(par_expm1, 1)
                pool.wait_ge(par_sin, 2)
                cos1, sin1, sinh1 = (angles[:, i * CH:(i + 1) * CH] for i in range(3))
                link(ts(tmp[2], sinh1, -2.0, None, ALU.mult))
                link(tt(out=tmp[2], in0=tmp[2], in1=sinh1, op=ALU.mult))
                link(tt(out=tmp[3], in0=expm1, in1=cos1, op=ALU.mult))
                link(tt(out=tmp[2], in0=tmp[2], in1=tmp[3], op=ALU.add))
                link(ts(tmp[3], expm1, 1.0, None, ALU.add))
                link(tt(out=tmp[3], in0=tmp[3], in1=sin1, op=ALU.mult))
                link(tt(out=tmp[4], in0=tmp[3], in1=w_im, op=ALU.mult))
                link(tt(out=tmp[5], in0=tmp[2], in1=a_re, op=ALU.mult))
                link(tt(out=tmp[4], in0=tmp[4], in1=tmp[5], op=ALU.subtract))
                link(tt(out=fr, in0=tmp[4], in1=inverse, op=ALU.mult))
                link(tt(out=tmp[4], in0=tmp[3], in1=a_re, op=ALU.mult))
                link(tt(out=tmp[5], in0=tmp[2], in1=w_im, op=ALU.mult))
                link(tt(out=tmp[4], in0=tmp[4], in1=tmp[5], op=ALU.add))
                link(ts(tmp[4], tmp[4], -1.0, None, ALU.mult))
                link(tt(out=fi, in0=tmp[4], in1=inverse, op=ALU.mult))

            over_ul = [ul[:, n * LH * CH:(n + 1) * LH * CH].rearrange("p (h a) -> p h a", a=LH) for n in range(2)]

            def far_factors():
                pool.wait_ge(par_exp, 1 + LH)
                for cs in range(2):
                    part = sn[:, cs * LH * CH:(cs + 1) * LH * CH]
                    link(tt(out=part, in0=part, in1=decays_a, op=ALU.mult))
                er = sn[:, 0:LH * CH].rearrange("p (a h) -> p h a", a=LH)
                ei = sn[:, LH * CH:2 * LH * CH].rearrange("p (a h) -> p h a", a=LH)
                m1, m2 = over_ul

                def over_a(t):
                    return t.unsqueeze(2).to_broadcast((P, CH, LH))

                link(tt(out=m1, in0=er, in1=over_a(fr), op=ALU.mult))
                link(tt(out=m2, in0=ei, in1=over_a(fi), op=ALU.mult))
                link(tt(out=x1[:, :, :], in0=m1, in1=m2, op=ALU.subtract))
                link(tt(out=m1, in0=er, in1=over_a(fi), op=ALU.mult))
                link(tt(out=m2, in0=ei, in1=over_a(fr), op=ALU.mult))
                link(tt(out=x2[:, :, :], in0=m1, in1=m2, op=ALU.add))

            def far_signs():
                top, low, m1 = slice(0, NS), slice(NS, P), over_ul[0]
                pool.wait_ge(h1b_ready, 7)
                link(ts(m1[low], x1[low, :, :], -2.0, None, ALU.mult))
                link(ts(x1[top, :, :], x1[top, :, :], 2.0, None, ALU.mult))
                link(ts(x2[:, :, :], x2[:, :, :], -2.0, None, ALU.mult))
                link(ts(x1[low, :, :], x2[low, :, :], 1.0, None, ALU.mult))
                link(ts(x2[low, :, :], m1[low], 1.0, None, ALU.mult))

            def prepare(s):
                if s < 3:
                    (exponentials_begun, exponentials, angle_args)[s]()
                if s > 3:
                    (wrapped, one_step_factor, far_factors, far_signs)[s - 4]()

            main_steps(step, prepare, chunk, pool.Fori)

        @block.scalar
        def _(act):
            def turn_out(dst, src, done, value, ready):
                act.wait_ge(done, value)
                act.activation(dst, src, ACT.Copy).then_inc(ready, 1)

            def flat(t):
                return t[:, :, :].rearrange("p c n -> p (c n)")

            def round_weight(n):
                act.wait_ge(w_loaded[n % STAGES], 16 * (n // STAGES + 1))
                if n < len(halves):
                    name, c = halves[n]
                    act.activation(w_hi[name][:, c:c + 2, :], w_stage[n % STAGES], ACT.Copy).then_inc(w_hi_ready, 1)
                else:
                    act.activation(up_hi[:, :], w_stage[UP_STAGE][:, 0, :], ACT.Copy).then_inc(w_hi_ready, 1)

            round_weight(0)
            turn_out(flat(x_hi), xt_bank[:, :], xt_done, 1, x_hi_ready)
            for n in range(1, 7):
                round_weight(n)

            def prepare(s):
                if s == 3:
                    act.wait_ge(par_args, 2)
                    act.activation(tanh_half, decay[:, :], ACT.Tanh, scale=0.5).then_inc(par_exp, 1)
                    for a in range(LH):
                        act.activation(decays_a[:, a * CH:(a + 1) * CH], decay[:, :], ACT.Exp,
                                       scale=float(a * P)).then_inc(par_exp, 1)
                if s == 4:
                    act.wait_ge(par_wrapped, 2)
                    act.activation(sn, sn, ACT.Sin, scale=SIN_SCALE).then_inc(par_sin, 1)
                    act.activation(angles, angles, ACT.Sin, scale=SIN_SCALE).then_inc(par_sin, 1)

            def chunk(i, u):
                if u == 0:
                    act.wait_ge(g_decay_args, i + 1)
                    act.activation(ex, ex, ACT.Exp).then_inc(g_exp, 1)
                if u == 1:
                    act.wait_ge(g_wrapped, i + 1)
                    act.activation(sn, sn, ACT.Sin, scale=-SIN_SCALE, bias=quarter[:, 1:2]).then_inc(g_sin, 1)
                if u == 2:
                    wait(act, tok_stored, i * (16 * 4 * LH))
                    for m in range(2):
                        act.wait_ge(g_mm, i * 2 + (m + 1))
                        act.activation(g_out[:, m, :], gen_bank[m][:, :], ACT.Copy).then_inc(g_evac, 1)

            def step(s, u):
                if has(s, s):
                    wait(act, s_done, s * G)
                    turn_out(k_hi[:, :], turn[:, :], k_turned, s + 1, k_hi_ready)
                    if known(s) and s == 0:
                        round_weight(7)
                        act.wait_ge(pads_zeroed, 2)
                    act.wait_ge(q_turned, s + 1)
                    for j in range(J):
                        act.activation(quarter_of(q_hi, j), by_group(turn, j), ACT.Copy).then_inc(q_hi_ready, 1)
                    if known(s) and s == 0:
                        for n in range(8, len(halves) + 1):
                            round_weight(n)
                    wait(act, pv_done, s)
                    turn_out(flat(v_rows), vt_bank[:, :], vt_done, s + 1, v_rows_ready)
                if has(s, s + 1):
                    turn_out(flat(x_hi), xt_bank[:, :], xt_done, s + 2, x_hi_ready)
                if has(s, s - 1):
                    turn_out(flat(x2_f), x2t_bank[:, :], x2t_done, s, x2_f_ready)
                    act.activation(flat(x2_hi), x2t_bank[:, :], ACT.Copy).then_inc(x2_hi_ready, 1)
                if has(s, s):
                    turn_out(flat(o_hi), ot_bank[:, :], ot_done, s + 1, o_hi_ready)
                if has(s, s - 1):
                    turn_out(hm_hi[:, :], x2t_bank[:, 0:P], hmt_done, s, hm_hi_ready)

            main_steps(step, prepare, chunk, act.Fori)

        @block.vector
        def _(dve):
            chain = [0, 0]

            def link(ins, meanwhile=None):
                chain[1] += 1
                ins.then_inc(dve_done, 1)
                if meanwhile:
                    meanwhile()
                dve.wait_ge(dve_done, chain[0] + chain[1])

            tt, ts, stt = dve.tensor_tensor, dve.tensor_scalar, dve.scalar_tensor_tensor

            def prepare(s):
                if s == 0:
                    dve.wait_ge(par_loaded, 96)
                    link(ts(k2, logs, LOG2E, MAGIC, ALU.mult, ALU.add))
                    link(ts(k2, k2, MAGIC, None, ALU.subtract))
                    link(ts(k2, k2, -126.0, 127.0, ALU.max, ALU.min))
                    ts(e2.bitcast(i32), k2, 127.0, 8388608.0, ALU.add, ALU.mult).then_inc(par_scales, 1)
                if s == 2:
                    dve.wait_ge(par_args, 1)
                    dve.reciprocal(inverse, tmp[0]).then_inc(par_inverse, 1)
                if s == 3:
                    dve.wait_ge(par_turns, 1)
                    ts(spare, angles, MAGIC, MAGIC, ALU.add, ALU.subtract)
                    ts(wraps[0], sn[:, 0:LH * CH], MAGIC, MAGIC, ALU.add, ALU.subtract)
                    ts(wraps[1], sn[:, LH * CH:], MAGIC, MAGIC, ALU.add, ALU.subtract).then_inc(par_rounded, 1)
                if s == 4:
                    dve.wait_ge(par_exp, 1)
                    link(ts(expm1, tanh_half, -1.0, 1.0, ALU.mult, ALU.add))
                    link(dve.reciprocal(expm1, expm1))
                    stt(out=expm1, in0=tanh_half, scalar=2.0, in1=expm1, op0=ALU.mult, op1=ALU.mult
                        ).then_inc(par_expm1, 1)

            def row_statistics(src):
                link(dve.bn_stats(stats[:, :], src))
                dve.memset(ln[:, 4:5], 0.0)
                link(dve.bn_aggr(mv[:, :], stats[:, :]))

            def normalized(src, dst, meanwhile=(None,) * 4):
                var, half, y, z = ln[:, 0:1], ln[:, 1:2], ln[:, 2:3], ln[:, 3:4]
                link(ts(var, mv[:, 1:2], EPS, None, ALU.add))
                ts(half, var, -0.5, None, ALU.mult)
                link(ts(y.bitcast(i32), var.bitcast(i32), -0.5, 1597463007.0, ALU.mult, ALU.add), meanwhile[0])
                for n in range(3):
                    link(stt(out=z, in0=y, scalar=half, in1=y, op0=ALU.mult, op1=ALU.mult), meanwhile[n + 1])
                    link(stt(out=y, in0=z, scalar=1.5, in1=y, op0=ALU.add, op1=ALU.mult))
                return ts(dst, src, mv[:, 0:1], y, ALU.subtract, ALU.mult)

            def layernorm(src, dst):
                row_statistics(src)
                return normalized(src, dst)

            def flat(t):
                return t[:, :, :].rearrange("p c n -> p (c n)")

            def rest(lo, bank_, hi, hi_ready, value, lo_ready):
                dve.wait_ge(hi_ready, value)
                tt(out=lo, in0=bank_, in1=hi.bitcast(f32), op=ALU.subtract).then_inc(lo_ready, 1)

            def turned(t):
                return t.rearrange("p (g h t) -> p h g t", g=G, t=TG)

            def heads(t):
                return t.rearrange("p (h g t) -> p h g t", h=H, g=G)

            def step(s, u):
                def split_queries(j):
                    rest(quarter_of(q_lo, j), by_group(turn, j), quarter_of(q_hi, j), q_hi_ready,
                         s * J + (j + 1), q_lo_ready)

                def turn_keys():
                    dve.wait_ge(k_done, s + 1)
                    wait(dve, s_done, s * G)
                    dve.transpose(turned(turn[:, :]), heads(k_bank[:, :])).then_inc(k_turned, 1)

                if has(s, s + 1) and not (known(s) and s == 0):
                    dve.wait_ge(xt_done, s + 1)
                    normalized(h_in[:, (u + 1) % 4, :], xn[:, :], [None, None, None, turn_keys]).then_inc(xn_ready, 1)
                elif has(s, s):
                    turn_keys()
                if has(s, s):
                    rest(k_lo[:, :], turn[:, :], k_hi[:, :], k_hi_ready, s + 1, k_lo_ready)
                    dve.wait_ge(k_lo_ready, s + 1)
                    dve.wait_ge(q_done, s + 1)
                    dve.transpose(turned(turn[:, :]), heads(q_bank[:, :])).then_inc(q_turned, 1)
                if has(s, s - 2):
                    dve.wait_ge(y_done, s - 1)
                    dve.wait_ge(h1b_ready, s - 1)
                    wait(dve, stored[u % 2], ((s // 2 - 1) * 16) if known(s) else s * 8 - (8 * (u % 2) + 16))
                    tt(out=out_sb[:, u % 2, :], in0=y_bank[:, :], in1=h1b[:, u % 2, :],
                       op=ALU.add).then_inc(out_ready, 1)
                if has(s, s):
                    for j in range(J - 1):
                        split_queries(j)

                def turn_values():
                    dve.wait_ge(v_done, s + 1)
                    wait(dve, vt_done, s)
                    dve.transpose(turned(v_turn[:, :]), heads(v_bank[:, :])).then_inc(v_turned, 1)
                    wait(dve, pv_done, s)

                def mask(g):
                    dve.wait_ge(s_done, s * G + (g + 1))
                    tt(out=probs[:, g, :], in0=s_bank[g][:, :], in1=diag[:, :], op=ALU.mult).then_inc(probs_ready, 1)

                attention = [turn_values, lambda: mask(0), lambda: mask(1), None]
                if has(s, s - 1):
                    b2, v = (u + 1) % 2, (u - 1) % 4
                    dve.wait_ge(wo_done, s)
                    if known(s) and s == 1:
                        dve.wait_ge(vob_lo_ready, 7)
                    tt(out=h1[:, b2, :], in0=wo_bank[:, :], in1=h_in[:, v, :], op=ALU.add).then_inc(h1_ready, 1)
                if has(s, s):
                    split_queries(J - 1)
                if has(s, s - 1):
                    dve.wait_ge(h1_ready, s)
                    wait(dve, x2t_done, s - 1)
                    row_statistics(h1[:, b2, :])
                    normalized(h1[:, b2, :], xn2[:, :], *([attention] if has(s, s) else [])).then_inc(xn2_ready, 1)
                elif has(s, s):
                    dve.wait_ge(h_loaded[1], 16)
                    dve.wait_ge(xt_done, 1)
                    row_statistics(h_in[:, 1, :])
                    normalized(h_in[:, 1, :], xn[:, :], attention).then_inc(xn_ready, 1)
                if has(s, s):
                    mask(2)
                    mask(3)
                if has(s, s + 1):
                    rest(flat(x_lo), xt_bank[:, :], flat(x_hi), x_hi_ready, s + 2, x_lo_ready)
                if has(s, s):
                    dve.wait_ge(pv_done, s + 1)
                    dve.transpose(o_tok[:, :], pv_bank[:, :]).then_inc(o_tok_ready, 1)
                if has(s, s - 1):
                    rest(flat(x2_lo), x2t_bank[:, :], flat(x2_hi), x2_hi_ready, s, x2_lo_ready)
                if has(s, s - 1):
                    dve.wait_ge(lora_done, s)
                    logits = lora_bank[:, P:P + EX]
                    link(dve.reduce_max(best[:, 0:1], logits, AX))
                    link(stt(out=ranked[:, :], in0=logits, scalar=best[:, 0:1], in1=prio[:, :],
                             op0=ALU.is_ge, op1=ALU.mult))
                    link(dve.reduce_max(best[:, 1:2], ranked[:, :], AX))
                    link(ts(onehot[:, :], ranked[:, :], best[:, 1:2], SCALING, ALU.is_equal, ALU.mult))
                    wait(dve, hmt_done, s - 1)
                    tt(out=hm[:, :].rearrange("p (e r) -> p e r", e=EX),
                       in0=lora_bank[:, 0:P].rearrange("p (e r) -> p e r", e=EX),
                       in1=onehot[:, :].unsqueeze(2).to_broadcast((P, EX, R)), op=ALU.mult).then_inc(hm_ready, 1)
                if has(s, s):
                    rest(flat(o_lo), ot_bank[:, :], flat(o_hi), o_hi_ready, s + 1, o_lo_ready)
                if has(s, s + 2):
                    v = (u + 2) % 4
                    dve.wait_ge(h_loaded[v], ((s + 2) // 4 + 1) * 16 if known(s) else (s + (2 - v)) * 4 + 16)
                    row_statistics(h_in[:, v, :])
                if has(s, s - 1):
                    rest(hm_lo[:, :], x2t_bank[:, 0:P], hm_hi[:, :], hm_hi_ready, s, hm_lo_ready)

            dve.wait_ge(h_loaded[0], 16)
            layernorm(h_in[:, 0, :], xn[:, :]).then_inc(xn_ready, 1)
            for n, (name, c) in enumerate(halves[0:4]):
                dve.wait_ge(w_hi_ready, n + 1)
                tt(out=w_lo[name][:, c:c + 2, :], in0=w_stage[n % STAGES],
                   in1=w_hi[name][:, c:c + 2, :].bitcast(f32), op=ALU.subtract).then_inc(qk_lo_ready, 1)
                if n == 0:
                    rest(flat(x_lo), xt_bank[:, :], flat(x_hi), x_hi_ready, 1, x_lo_ready)

            dve.wait_ge(consts_made, 7)
            di = probs[:, 0, :]
            link(ts(di, diag[:, :], 1.0 / TG, None, ALU.mult))
            link(ts(probs[:, 1, :], di, MAGIC, MAGIC, ALU.add, ALU.subtract))
            link(tt(out=diag[:, :], in0=di, in1=probs[:, 1, :], op=ALU.is_equal))

            @contextmanager
            def linked_loop(first, last):
                before = chain[0] + chain[1]
                with dve.Fori(first, last) as it:
                    chain[:] = [before + (it - first) * LINKS, 0]
                    yield it
                    assert chain[1] == LINKS, chain[1]
                chain[:] = [before + (last - first) * LINKS, 0]

            LINKS = 4 * 24
            main_steps(step, prepare, lambda i, u: None, linked_loop)

        @block.tensor
        def _(pe):
            def transposes(bank_, src):
                for c in range(NC_):
                    last = pe.transpose(bank_[:, c * P:(c + 1) * P], src[:, c * P:(c + 1) * P], ident[:, :])
                return last

            def project(bank_, hi, lo, name, stop=True, lo_ready=None, value=None):
                products = [(hi, w_hi[name]), (hi, w_lo[name]), (lo, w_hi[name])]
                for n, (x, w) in enumerate(products):
                    if n == 2 and lo_ready:
                        pe.wait_ge(lo_ready, value)
                    for c in range(NC_):
                        last = pe.matmul(bank_[:, :], x[:, c, :], w[:, c, :], start=(n == 0 and c == 0),
                                         stop=(stop and n == 2 and c == NC_ - 1))
                return last

            waits_evac = [None]

            def chunk(i, u):
                if u != 2:
                    return
                pe.wait_ge(g_g, i + 1)
                pe.wait_ge(g_e2, i + 1)
                for m in range(2):
                    for c in range(8):
                        ch = 8 * m + c
                        rows = slice(64 * (c % 2), 64 * (c % 2) + 64)
                        last = pe.matmul(gen_bank[m][rows, (c // 2) * P:(c // 2 + 1) * P],
                                         gbuf[:, 0, ch, :, :].rearrange("p a b -> p (a b)"),
                                         ex[:, ch * P:(ch + 1) * P], start=True, stop=True)
                    last.then_inc(g_mm, 1)
                waits_evac[0] = i

            pe.wait_ge(ident_made, 2)
            pe.wait_ge(xn_ready, 1)
            transposes(xt_bank, xn).then_inc(xt_done, 1)

            def step(s, u):
                if has(s, s):
                    pe.wait_ge(x_hi_ready, s + 1)
                    if known(s) and s == 0:
                        pe.wait_ge(qk_lo_ready, 2)
                    project(k_bank, x_hi, x_lo, "k", lo_ready=x_lo_ready, value=s + 1).then_inc(k_done, 1)
                if has(s, s - 1):
                    pe.wait_ge(o_hi_ready, s)
                    pe.wait_ge(o_lo_ready, s)
                if has(s, s):
                    if known(s) and s == 0:
                        pe.wait_ge(qk_lo_ready, 4)
                    project(q_bank, x_hi, x_lo, "q").then_inc(q_done, 1)
                if has(s, s - 2):
                    pe.wait_ge(hm_hi_ready, s - 1)
                    pe.wait_ge(hm_lo_ready, s - 1)
                    pe.matmul(y_bank[:, :], hm_hi[:, :], up_hi[:, :], start=False, stop=False)
                    pe.matmul(y_bank[:, :], hm_hi[:, :], up_lo[:, :], start=False, stop=False)
                    pe.matmul(y_bank[:, :], hm_lo[:, :], up_hi[:, :], start=False, stop=True).then_inc(y_done, 1)
                if has(s, s - 1):
                    if known(s) and s == 1:
                        pe.wait_ge(vob_lo_ready, 7)
                        pe.wait_ge(small_loaded, 48)
                    project(wo_bank, o_hi, o_lo, "o").then_inc(wo_done, 1)
                if waits_evac[0] is not None:
                    pe.wait_ge(g_evac, waits_evac[0] * 2 + 2)
                    waits_evac[0] = None
                if has(s, s):
                    if known(s) and s == 0:
                        pe.wait_ge(vob_lo_ready, 2)
                    project(v_bank, x_hi, x_lo, "v").then_inc(v_done, 1)
                if has(s, s):
                    pe.wait_ge(k_lo_ready, s + 1)
                    pe.wait_ge(q_hi_ready, s * J + J)
                    for g in range(G):
                        if g == G - 1:
                            pe.wait_ge(v_turned, s + 1)
                            transposes(vt_bank, v_turn).then_inc(vt_done, 1)
                        for n, (k, q) in enumerate(((k_hi, q_hi), (k_lo, q_hi), (k_hi, q_lo))):
                            if g == 0 and n == 2:
                                pe.wait_ge(q_lo_ready, s * J + J)
                            last = pe.matmul(s_bank[g][:, :], k[:, g * P:(g + 1) * P], q[:, g, :],
                                             start=(n == 0), stop=(n == 2))
                        last.then_inc(s_done, 1)
                if has(s, s + 1):
                    pe.wait_ge(xn_ready, s + 2)
                    wait(pe, probs_ready, s * G + 2)
                    transposes(xt_bank, xn).then_inc(xt_done, 1)
                for g in range(G):
                    if g == 1 and has(s, s - 1):
                        pe.wait_ge(xn2_ready, s)
                        transposes(x2t_bank, xn2).then_inc(x2t_done, 1)
                    if has(s, s):
                        if g == 0:
                            pe.wait_ge(v_rows_ready, s + 1)
                        pe.wait_ge(probs_ready, s * G + (g + 1))
                        for j in range(J):
                            dst = pv_bank[DK * j:DK * j + DK, :].rearrange("p (h g t) -> p h g t", h=H, g=G)
                            last = pe.matmul(dst[:, :, g, :], v_rows[:, g, DK * j:DK * j + DK],
                                             probs[:, g, j * P:(j + 1) * P], start=True, stop=True)
                if has(s, s):
                    last.then_inc(pv_done, 1)
                if has(s, s - 1):
                    pe.wait_ge(x2_f_ready, s)
                    for c in range(NC_):
                        last = pe.matmul(lora_bank[:, 0:P + EX], x2_f[:, c, :], ar[:, c, :], start=(c == 0),
                                         stop=(c == NC_ - 1))
                    last.then_inc(lora_done, 1)
                if has(s, s):
                    pe.wait_ge(o_tok_ready, s + 1)
                    transposes(ot_bank, o_tok).then_inc(ot_done, 1)
                if has(s, s - 1):
                    wait(pe, out_ready, s - 1)
                    pe.wait_ge(x2_hi_ready, s)
                    project(y_bank, x2_hi, x2_lo, "b", stop=False, lo_ready=x2_lo_ready, value=s)
                    pe.wait_ge(hm_ready, s)
                    pe.transpose(x2t_bank[:, 0:P], hm[:, :], ident[:, :]).then_inc(hmt_done, 1)

            main_steps(step, lambda u: None, chunk, pe.Fori)


def kernel(x, txt, L0_tok_log_dt, L0_tok_log_w_real, L0_tok_w_imag, L0_attn_Wq, L0_attn_Wk, L0_attn_Wv,
           L0_attn_Wo, L0_ffn_W_base, L0_ffn_b_base, L0_ffn_router_W, L0_ffn_A, L0_ffn_Bw):
    import concourse.bacc as bacc
    from concourse.bass_utils import run_bass_kernel_spmd

    def laid(a):
        return np.ascontiguousarray(a)

    arrays = {
        "c_parts": laid(np.transpose(np.asarray(x), (3, 2, 1, 0))),
        "txt": laid(txt),
        "log_dt": laid(L0_tok_log_dt),
        "log_w_real_t": laid(np.transpose(np.asarray(L0_tok_log_w_real))),
        "w_imag_t": laid(np.transpose(np.asarray(L0_tok_w_imag))),
        "wq": laid(L0_attn_Wq), "wk": laid(L0_attn_Wk), "wv": laid(L0_attn_Wv), "wo": laid(L0_attn_Wo),
        "w_base_t": laid(np.transpose(np.asarray(L0_ffn_W_base))),
        "b_base": laid(L0_ffn_b_base),
        "router_t": laid(np.transpose(np.asarray(L0_ffn_router_W))),
        "a_t": laid(np.transpose(np.asarray(L0_ffn_A).reshape(EX * R, D))),
        "bw_t": laid(np.transpose(np.asarray(L0_ffn_Bw), (0, 2, 1)).reshape(EX * R, D)),
    }
    nc = bacc.Bacc("TRN2", target_bir_lowering=False, num_devices=1)
    args = [nc.dram_tensor(f"in_{n}", a.shape, mybir.dt.from_np(a.dtype), kind="ExternalInput").ap()
            for n, a in arrays.items()]
    out = nc.dram_tensor("out_rows", (B, ROWS, D), mybir.dt.float32, kind="ExternalOutput").ap()
    fusion_kernel(nc, *args, out)
    r = run_bass_kernel_spmd(nc, [{f"in_{n}": a for n, a in arrays.items()}], core_ids=[0])
    return r.results[0]["out_rows"]
```
